# Optimizing a Trainium2 kernel written in Bass

```python
import numpy as np
import jax
import jax.numpy as jnp

def _softmax(x, axis=-1):
    return jax.nn.softmax(x, axis=axis)

def _gelu(x):
    return jax.nn.gelu(x, approximate=True)

def _silu(x):
    return jax.nn.silu(x)

def _sigmoid(x):
    return jax.nn.sigmoid(x)

def _layernorm(x, axis=-1, eps=1e-05):
    m = jnp.mean(x, axis=axis, keepdims=True)
    v = jnp.var(x, axis=axis, keepdims=True)
    return (x - m) / jnp.sqrt(v + eps)

def _scatter_add(tgt, idx, src, axis=0):
    return tgt.at[idx].add(src)

def _segment_sum(src, seg, n):
    return jax.ops.segment_sum(src, seg, n)
kernel_name = 'mk_adj_ffn_d2_adj_r2_ea1061'

def setup_inputs(seed: int=0):
    np.random.seed(seed)
    _w = jnp.asarray

    def _rec_inputs():
        import jax
        import jax.numpy as jnp
        _gk = jax.random.key(seed)
        x = -0.0002422 + 1 * jax.random.normal(jax.random.fold_in(_gk, 1), (64, 128, 128), jnp.float32)
        _a = jax.random.bernoulli(jax.random.fold_in(_gk, 2), 0.125, (64, 128, 128))
        adj = _a.astype(jnp.int32)
        return (x, adj)
    x, adj = _rec_inputs()

    def _L0_gnn_setup():
        import jax, jax.numpy as jnp
        import numpy as np
        NEG_INF = -9000000000000000.0
        LEAKY_SLOPE = 0.2
        key = jax.random.key(seed)
        k1, k2, k3, k4, k5, k6 = jax.random.split(key, 6)
        B, N, D = (256, 200, 128)
        hidden = jax.random.normal(k1, (B, N, D), dtype=jnp.float32)
        adj = jax.random.randint(k2, (B, N, N), 0, 5, dtype=jnp.int32)
        a0 = jax.random.normal(k3, (D,), dtype=jnp.float32)
        a1 = jax.random.normal(k4, (D,), dtype=jnp.float32)
        a2 = jax.random.normal(k5, (D,), dtype=jnp.float32)
        a3 = jax.random.normal(k6, (D,), dtype=jnp.float32)
        return {'hidden': hidden, 'adj': adj, 'a0': a0, 'a1': a1, 'a2': a2, 'a3': a3}
    _L0_gnn_all = _L0_gnn_setup()
    _L0_gnn_in = {k: v for k, v in _L0_gnn_all.items() if k in ('a0', 'a1', 'a2', 'a3')}
    del _L0_gnn_all

    def _L0_ffn_setup():
        import jax, jax.numpy as jnp
        import numpy as np
        DIM = 128
        HEADS = 8
        NUM_KEYS = 128
        NUM_KV = NUM_KEYS ** 2
        PK_TOPK = 16
        FINAL_TOPK = 16
        DIM_KEY = DIM // 2
        P = 2

        def _pk(x, Wq_pk, pk_keys):
            b, n, _ = x.shape
            q = (x @ Wq_pk).reshape(b, n, P, HEADS, DIM_KEY).transpose(2, 0, 1, 3, 4)
            sim = jnp.einsum('pbnhd,pkhd->pbnhk', q, pk_keys)
            scores, idx = jax.lax.top_k(sim, PK_TOPK)
            idx0 = idx[0]
            idx1 = idx[1] * NUM_KEYS
            index = (idx0[..., :, None] + idx1[..., None, :]).reshape(b, n, HEADS, PK_TOPK * PK_TOPK)
            score = (scores[0][..., :, None] + scores[1][..., None, :]).reshape(b, n, HEADS, PK_TOPK * PK_TOPK)
            final_scores, pk_idx = jax.lax.top_k(score, FINAL_TOPK)
            final_indices = jnp.take_along_axis(index, pk_idx, axis=-1)
            final_scores = jax.nn.softmax(final_scores, axis=-1)
            return (final_scores, final_indices)
        key = jax.random.key(seed)
        ks = jax.random.split(key, 7)
        b, n = (2, 512)
        std = 0.02
        x = jax.random.normal(ks[0], (b, n, DIM), dtype=jnp.float32)
        Wq_pk = jax.random.normal(ks[1], (DIM, P * HEADS * DIM_KEY), dtype=jnp.float32) * std
        pk_keys = jax.random.normal(ks[2], (P, NUM_KEYS, HEADS, DIM_KEY), dtype=jnp.float32) * std
        Wq = jax.random.normal(ks[3], (DIM, HEADS * DIM), dtype=jnp.float32) * std
        keys_table = jax.random.normal(ks[4], (NUM_KV * HEADS, DIM), dtype=jnp.float32) * std
        values_table = jax.random.normal(ks[5], (NUM_KV * HEADS, DIM), dtype=jnp.float32) * std
        Wo = jax.random.normal(ks[6], (DIM * HEADS, DIM), dtype=jnp.float32) * std
        return {'x': x, 'Wq_pk': Wq_pk, 'pk_keys': pk_keys, 'Wq': Wq, 'keys_table': keys_table, 'values_table': values_table, 'Wo': Wo}
    _L0_ffn_all = _L0_ffn_setup()
    _L0_ffn_in = {k: v for k, v in _L0_ffn_all.items() if k in ('Wq_pk', 'pk_keys', 'Wq', 'keys_table', 'values_table', 'Wo')}
    del _L0_ffn_all

    def _L1_gnn_setup():
        import jax, jax.numpy as jnp
        import numpy as np
        B, N, D, H = (4, 1024, 128, 8)
        HD = D // H
        DFF = 4 * D
        EPS = 1e-05

        def layer_norm(x, gamma, beta):
            mu = jnp.mean(x, axis=-1, keepdims=True)
            var = jnp.mean(jnp.square(x - mu), axis=-1, keepdims=True)
            return (x - mu) * jax.lax.rsqrt(var + EPS) * gamma + beta
        key = jax.random.key(seed)
        ks = jax.random.split(key, 10)
        x = jax.random.normal(ks[0], (B, N, D), dtype=jnp.float32)
        adj = jax.random.randint(ks[1], (B, N, N), 0, 2).astype(jnp.int32)
        idx = jnp.arange(N)
        adj = adj.at[:, idx, idx].set(1)
        gamma1 = 1.0 + 0.02 * jax.random.normal(ks[2], (D,), dtype=jnp.float32)
        beta1 = 0.02 * jax.random.normal(ks[3], (D,), dtype=jnp.float32)
        gamma2 = 1.0 + 0.02 * jax.random.normal(ks[4], (D,), dtype=jnp.float32)
        beta2 = 0.02 * jax.random.normal(ks[5], (D,), dtype=jnp.float32)
        W1 = 0.02 * jax.random.normal(ks[6], (D, DFF), dtype=jnp.float32)
        b1 = 0.01 * jax.random.normal(ks[7], (DFF,), dtype=jnp.float32)
        W2 = 0.02 * jax.random.normal(ks[8], (DFF, D), dtype=jnp.float32)
        b2 = 0.01 * jax.random.normal(ks[9], (D,), dtype=jnp.float32)
        return {'x': x, 'adj_matrix': adj, 'gamma1': gamma1, 'beta1': beta1, 'gamma2': gamma2, 'beta2': beta2, 'W1': W1, 'b1': b1, 'W2': W2, 'b2': b2}
    _L1_gnn_all = _L1_gnn_setup()
    _L1_gnn_in = {k: v for k, v in _L1_gnn_all.items() if k in ('gamma1', 'beta1', 'gamma2', 'beta2', 'W1', 'b1', 'W2', 'b2')}
    del _L1_gnn_all

    def _L1_ffn_setup():
        import jax, jax.numpy as jnp
        import numpy as np
        H, P, G, NS, K = (8, 64, 64, 64, 3)
        D_INNER = H * P
        CONV_DIM = D_INNER + 2 * NS
        D_IN_PROJ = 2 * D_INNER + 2 * NS + 2 * H

        def _hydra(u, in_w, conv_w, conv_b, dt_bias, A_log, Dp, fcD_w, norm_w, out_w):
            Bt, L, _ = u.shape
            zxbcdt = u @ in_w.T
            z = zxbcdt[..., :D_INNER]
            xBC = zxbcdt[..., D_INNER:D_INNER + CONV_DIM]
            dt = zxbcdt[..., -2 * H:]
            dt = jnp.concatenate([dt[..., :H], jnp.flip(dt[..., H:], axis=1)], axis=0)
            dt = jax.nn.softplus(dt + dt_bias)
            xp = jnp.pad(xBC, ((0, 0), (K - 1, 0), (0, 0)))
            xBC = sum((xp[:, k:k + L, :] * conv_w[:, k] for k in range(K))) + conv_b
            xBC = jax.nn.silu(xBC)
            x = xBC[..., :D_INNER]
            Bm = xBC[..., D_INNER:D_INNER + NS]
            Cm = xBC[..., D_INNER + NS:]
            x_og = x
            x2 = jnp.concatenate([x, jnp.flip(x, 1)], 0).reshape(2 * Bt, L, H, P)
            B2 = jnp.concatenate([Bm, jnp.flip(Bm, 1)], 0)
            C2 = jnp.concatenate([Cm, jnp.flip(Cm, 1)], 0)
            dA = jnp.exp(dt * -jnp.exp(A_log))
            dBx = jnp.einsum('blh,bln,blhp->blhpn', dt, B2, x2)

            def step(h, inp):
                dA_t, dBx_t, C_t = inp
                h = h * dA_t[:, :, None, None] + dBx_t
                return (h, jnp.einsum('bhpn,bn->bhp', h, C_t))
            h0 = jnp.zeros((2 * Bt, H, P, NS), u.dtype)
            _, ys = jax.lax.scan(step, h0, (dA.transpose(1, 0, 2), dBx.transpose(1, 0, 2, 3, 4), C2.transpose(1, 0, 2)))
            y = ys.transpose(1, 0, 2, 3).reshape(2 * Bt, L, D_INNER)
            y_fw, y_bw = (y[:Bt], jnp.flip(y[Bt:], 1))
            y = jnp.pad(y_fw[:, :-1], ((0, 0), (1, 0), (0, 0))) + jnp.pad(y_bw[:, 1:], ((0, 0), (0, 1), (0, 0)))
            y = y + x_og * jnp.repeat(x_og @ fcD_w.T + Dp, P, axis=-1)
            yg = y * jax.nn.silu(z)
            yg = yg * jax.lax.rsqrt(jnp.mean(jnp.square(yg), -1, keepdims=True) + 1e-05) * norm_w
            return yg @ out_w.T
        key = jax.random.key(seed)
        ks = jax.random.split(key, 10)
        dim, Bsz, N = (128, 4, 4096)
        s = 0.02
        return {'x': jax.random.normal(ks[0], (Bsz, N, dim), jnp.float32), 'W_fx': jax.random.normal(ks[1], (D_INNER, dim), jnp.float32) * s, 'b_fx': jnp.zeros((D_INNER,), jnp.float32), 'W_x': jax.random.normal(ks[2], (D_INNER, dim), jnp.float32) * s, 'b_x': jnp.zeros((D_INNER,), jnp.float32), 'W_slice': jax.random.normal(ks[3], (G, P), jnp.float32) * s, 'b_slice': jnp.zeros((G,), jnp.float32), 'temperature': jnp.full((1, H, 1, 1), 0.5, jnp.float32), 'hy_in_w': jax.random.normal(ks[4], (D_IN_PROJ, D_INNER), jnp.float32) * s, 'hy_conv_w': jax.random.normal(ks[5], (CONV_DIM, K), jnp.float32) * s, 'hy_conv_b': jnp.zeros((CONV_DIM,), jnp.float32), 'hy_dt_bias': jnp.log(jnp.expm1(jnp.full((H,), 0.01, jnp.float32))), 'hy_A_log': jnp.log(jnp.linspace(1.0, 16.0, H)).astype(jnp.float32), 'hy_D': jnp.ones((H,), jnp.float32), 'hy_fcD_w': jax.random.normal(ks[6], (H, D_INNER), jnp.float32) * s, 'hy_norm_w': jnp.ones((D_INNER,), jnp.float32), 'hy_out_w': jax.random.normal(ks[7], (D_INNER, D_INNER), jnp.float32) * s, 'out_w': jax.random.normal(ks[8], (dim, D_INNER), jnp.float32) * s, 'out_b': jnp.zeros((dim,), jnp.float32)}
    _L1_ffn_all = _L1_ffn_setup()
    _L1_ffn_in = {k: v for k, v in _L1_ffn_all.items() if k in ('W_fx', 'b_fx', 'W_x', 'b_x', 'W_slice', 'b_slice', 'temperature', 'hy_in_w', 'hy_conv_w', 'hy_conv_b', 'hy_dt_bias', 'hy_A_log', 'hy_D', 'hy_fcD_w', 'hy_norm_w', 'hy_out_w', 'out_w', 'out_b')}
    del _L1_ffn_all
    return {'x': x, 'adj': adj, 'L0_gnn_a0': _L0_gnn_in['a0'], 'L0_gnn_a1': _L0_gnn_in['a1'], 'L0_gnn_a2': _L0_gnn_in['a2'], 'L0_gnn_a3': _L0_gnn_in['a3'], 'L0_ffn_Wq_pk': _L0_ffn_in['Wq_pk'], 'L0_ffn_pk_keys': _L0_ffn_in['pk_keys'], 'L0_ffn_Wq': _L0_ffn_in['Wq'], 'L0_ffn_keys_table': _L0_ffn_in['keys_table'], 'L0_ffn_values_table': _L0_ffn_in['values_table'], 'L0_ffn_Wo': _L0_ffn_in['Wo'], 'L1_gnn_gamma1': _L1_gnn_in['gamma1'], 'L1_gnn_beta1': _L1_gnn_in['beta1'], 'L1_gnn_gamma2': _L1_gnn_in['gamma2'], 'L1_gnn_beta2': _L1_gnn_in['beta2'], 'L1_gnn_W1': _L1_gnn_in['W1'], 'L1_gnn_b1': _L1_gnn_in['b1'], 'L1_gnn_W2': _L1_gnn_in['W2'], 'L1_gnn_b2': _L1_gnn_in['b2'], 'L1_ffn_W_fx': _L1_ffn_in['W_fx'], 'L1_ffn_b_fx': _L1_ffn_in['b_fx'], 'L1_ffn_W_x': _L1_ffn_in['W_x'], 'L1_ffn_b_x': _L1_ffn_in['b_x'], 'L1_ffn_W_slice': _L1_ffn_in['W_slice'], 'L1_ffn_b_slice': _L1_ffn_in['b_slice'], 'L1_ffn_temperature': _L1_ffn_in['temperature'], 'L1_ffn_hy_in_w': _L1_ffn_in['hy_in_w'], 'L1_ffn_hy_conv_w': _L1_ffn_in['hy_conv_w'], 'L1_ffn_hy_conv_b': _L1_ffn_in['hy_conv_b'], 'L1_ffn_hy_dt_bias': _L1_ffn_in['hy_dt_bias'], 'L1_ffn_hy_A_log': _L1_ffn_in['hy_A_log'], 'L1_ffn_hy_D': _L1_ffn_in['hy_D'], 'L1_ffn_hy_fcD_w': _L1_ffn_in['hy_fcD_w'], 'L1_ffn_hy_norm_w': _L1_ffn_in['hy_norm_w'], 'L1_ffn_hy_out_w': _L1_ffn_in['hy_out_w'], 'L1_ffn_out_w': _L1_ffn_in['out_w'], 'L1_ffn_out_b': _L1_ffn_in['out_b']}

def reference(x, adj, L0_gnn_a0, L0_gnn_a1, L0_gnn_a2, L0_gnn_a3, L0_ffn_Wq_pk, L0_ffn_pk_keys, L0_ffn_Wq, L0_ffn_keys_table, L0_ffn_values_table, L0_ffn_Wo, L1_gnn_gamma1, L1_gnn_beta1, L1_gnn_gamma2, L1_gnn_beta2, L1_gnn_W1, L1_gnn_b1, L1_gnn_W2, L1_gnn_b2, L1_ffn_W_fx, L1_ffn_b_fx, L1_ffn_W_x, L1_ffn_b_x, L1_ffn_W_slice, L1_ffn_b_slice, L1_ffn_temperature, L1_ffn_hy_in_w, L1_ffn_hy_conv_w, L1_ffn_hy_conv_b, L1_ffn_hy_dt_bias, L1_ffn_hy_A_log, L1_ffn_hy_D, L1_ffn_hy_fcD_w, L1_ffn_hy_norm_w, L1_ffn_hy_out_w, L1_ffn_out_w, L1_ffn_out_b):
    import jax
    import jax.numpy as jnp

    def _L0_gnn_ref(hidden, adj, a0, a1, a2, a3):
        import jax, jax.numpy as jnp
        import numpy as np
        NEG_INF = -9000000000000000.0
        LEAKY_SLOPE = 0.2

        def edge_score(a):
            s = jnp.einsum('bid,bjd->bij', hidden * a, hidden)
            return jax.nn.leaky_relu(s, LEAKY_SLOPE)
        e0, e1, e2, e3 = (edge_score(a0), edge_score(a1), edge_score(a2), edge_score(a3))
        alpha = jnp.where(adj == 1, e0, NEG_INF)
        alpha = jnp.where(adj == 2, e1, alpha)
        alpha = jnp.where(adj == 3, e2, alpha)
        alpha = jnp.where(adj == 4, e3, alpha)
        alpha = jax.nn.softmax(alpha, axis=-1)
        return jnp.matmul(alpha, hidden)

    def _L0_ffn_ref(x, Wq_pk, pk_keys, Wq, keys_table, values_table, Wo):
        import jax, jax.numpy as jnp
        import numpy as np
        DIM = 128
        HEADS = 8
        NUM_KEYS = 128
        NUM_KV = NUM_KEYS ** 2
        PK_TOPK = 16
        FINAL_TOPK = 16
        DIM_KEY = DIM // 2
        P = 2

        def _pk(x, Wq_pk, pk_keys):
            b, n, _ = x.shape
            q = (x @ Wq_pk).reshape(b, n, P, HEADS, DIM_KEY).transpose(2, 0, 1, 3, 4)
            sim = jnp.einsum('pbnhd,pkhd->pbnhk', q, pk_keys)
            scores, idx = jax.lax.top_k(sim, PK_TOPK)
            idx0 = idx[0]
            idx1 = idx[1] * NUM_KEYS
            index = (idx0[..., :, None] + idx1[..., None, :]).reshape(b, n, HEADS, PK_TOPK * PK_TOPK)
            score = (scores[0][..., :, None] + scores[1][..., None, :]).reshape(b, n, HEADS, PK_TOPK * PK_TOPK)
            final_scores, pk_idx = jax.lax.top_k(score, FINAL_TOPK)
            final_indices = jnp.take_along_axis(index, pk_idx, axis=-1)
            final_scores = jax.nn.softmax(final_scores, axis=-1)
            return (final_scores, final_indices)
        b, n, d = x.shape
        q = (x @ Wq).reshape(b, n, HEADS, DIM) * DIM ** (-0.5)
        kv_scores, indices = _pk(x, Wq_pk, pk_keys)
        offsets = jnp.arange(HEADS, dtype=indices.dtype) * NUM_KV
        ind = indices + offsets[None, None, :, None]
        k = jnp.einsum('bnhk,bnhkd->bnhd', kv_scores, keys_table[ind])
        v = jnp.einsum('bnhk,bnhkd->bnhd', kv_scores, values_table[ind])
        sim = jnp.einsum('bihd,bjhd->bhij', q, k)
        neg = -jnp.finfo(sim.dtype).max
        causal = jnp.tril(jnp.ones((n, n), dtype=bool))
        sim = jnp.where(causal, sim, neg)
        attn = jax.nn.softmax(sim, axis=-1)
        out = jnp.einsum('bhij,bjhd->bhid', attn, v)
        out = out.transpose(0, 2, 1, 3).reshape(b, n, HEADS * DIM)
        return out @ Wo

    def _L1_gnn_ref(x, adj_matrix, gamma1, beta1, gamma2, beta2, W1, b1, W2, b2):
        import jax, jax.numpy as jnp
        import numpy as np
        B, N, D, H = (4, 1024, 128, 8)
        HD = D // H
        DFF = 4 * D
        EPS = 1e-05

        def layer_norm(x, gamma, beta):
            mu = jnp.mean(x, axis=-1, keepdims=True)
            var = jnp.mean(jnp.square(x - mu), axis=-1, keepdims=True)
            return (x - mu) * jax.lax.rsqrt(var + EPS) * gamma + beta
        b_, n_, d_ = x.shape
        normed = layer_norm(x, gamma1, beta1)
        qkv = normed.reshape(b_, n_, H, HD).transpose(0, 2, 1, 3)
        scale = 1.0 / jnp.sqrt(jnp.asarray(HD, dtype=x.dtype))
        scores = jnp.einsum('bhqd,bhkd->bhqk', qkv, qkv) * scale
        mask = adj_matrix[:, None, :, :] > 0
        masked = jnp.where(mask, scores, -jnp.inf)
        attn = jax.nn.softmax(masked, axis=-1)
        out = jnp.einsum('bhqk,bhkd->bhqd', attn, qkv)
        out = out.transpose(0, 2, 1, 3).reshape(b_, n_, d_)
        x = x + out
        y = layer_norm(x, gamma2, beta2)
        mlp = jax.nn.gelu(y @ W1 + b1, approximate=False) @ W2 + b2
        return x + mlp

    def _L1_ffn_ref(x, W_fx, b_fx, W_x, b_x, W_slice, b_slice, temperature, hy_in_w, hy_conv_w, hy_conv_b, hy_dt_bias, hy_A_log, hy_D, hy_fcD_w, hy_norm_w, hy_out_w, out_w, out_b):
        import jax, jax.numpy as jnp
        import numpy as np
        H, P, G, NS, K = (8, 64, 64, 64, 3)
        D_INNER = H * P
        CONV_DIM = D_INNER + 2 * NS
        D_IN_PROJ = 2 * D_INNER + 2 * NS + 2 * H

        def _hydra(u, in_w, conv_w, conv_b, dt_bias, A_log, Dp, fcD_w, norm_w, out_w):
            Bt, L, _ = u.shape
            zxbcdt = u @ in_w.T
            z = zxbcdt[..., :D_INNER]
            xBC = zxbcdt[..., D_INNER:D_INNER + CONV_DIM]
            dt = zxbcdt[..., -2 * H:]
            dt = jnp.concatenate([dt[..., :H], jnp.flip(dt[..., H:], axis=1)], axis=0)
            dt = jax.nn.softplus(dt + dt_bias)
            xp = jnp.pad(xBC, ((0, 0), (K - 1, 0), (0, 0)))
            xBC = sum((xp[:, k:k + L, :] * conv_w[:, k] for k in range(K))) + conv_b
            xBC = jax.nn.silu(xBC)
            x = xBC[..., :D_INNER]
            Bm = xBC[..., D_INNER:D_INNER + NS]
            Cm = xBC[..., D_INNER + NS:]
            x_og = x
            x2 = jnp.concatenate([x, jnp.flip(x, 1)], 0).reshape(2 * Bt, L, H, P)
            B2 = jnp.concatenate([Bm, jnp.flip(Bm, 1)], 0)
            C2 = jnp.concatenate([Cm, jnp.flip(Cm, 1)], 0)
            dA = jnp.exp(dt * -jnp.exp(A_log))
            dBx = jnp.einsum('blh,bln,blhp->blhpn', dt, B2, x2)

            def step(h, inp):
                dA_t, dBx_t, C_t = inp
                h = h * dA_t[:, :, None, None] + dBx_t
                return (h, jnp.einsum('bhpn,bn->bhp', h, C_t))
            h0 = jnp.zeros((2 * Bt, H, P, NS), u.dtype)
            _, ys = jax.lax.scan(step, h0, (dA.transpose(1, 0, 2), dBx.transpose(1, 0, 2, 3, 4), C2.transpose(1, 0, 2)))
            y = ys.transpose(1, 0, 2, 3).reshape(2 * Bt, L, D_INNER)
            y_fw, y_bw = (y[:Bt], jnp.flip(y[Bt:], 1))
            y = jnp.pad(y_fw[:, :-1], ((0, 0), (1, 0), (0, 0))) + jnp.pad(y_bw[:, 1:], ((0, 0), (0, 1), (0, 0)))
            y = y + x_og * jnp.repeat(x_og @ fcD_w.T + Dp, P, axis=-1)
            yg = y * jax.nn.silu(z)
            yg = yg * jax.lax.rsqrt(jnp.mean(jnp.square(yg), -1, keepdims=True) + 1e-05) * norm_w
            return yg @ out_w.T
        B, N, _ = x.shape
        fx = (x @ W_fx.T + b_fx).reshape(B, N, H, P).transpose(0, 2, 1, 3)
        xm = (x @ W_x.T + b_x).reshape(B, N, H, P).transpose(0, 2, 1, 3)
        temp = jnp.maximum(temperature, 1e-06)
        sw = jax.nn.softmax((xm @ W_slice.T + b_slice) / temp, axis=-1)
        snorm = sw.sum(2)
        st = jnp.einsum('bhnc,bhng->bhgc', fx, sw) / (snorm + 1e-05)[..., None]
        st = st.transpose(0, 2, 1, 3).reshape(B, G, D_INNER)
        ot = _hydra(st, hy_in_w, hy_conv_w, hy_conv_b, hy_dt_bias, hy_A_log, hy_D, hy_fcD_w, hy_norm_w, hy_out_w)
        ot = ot.reshape(B, G, H, P).transpose(0, 2, 1, 3)
        out = jnp.einsum('bhgc,bhng->bhnc', ot, sw).transpose(0, 2, 1, 3).reshape(B, N, D_INNER)
        return out @ out_w.T + out_b
    x = x + _L0_gnn_ref(_layernorm(x, axis=-1), adj, L0_gnn_a0, L0_gnn_a1, L0_gnn_a2, L0_gnn_a3)
    x = x + _L0_ffn_ref(_layernorm(x, axis=-1), L0_ffn_Wq_pk, L0_ffn_pk_keys, L0_ffn_Wq, L0_ffn_keys_table, L0_ffn_values_table, L0_ffn_Wo)
    x = x + _L1_gnn_ref(_layernorm(x, axis=-1), adj, L1_gnn_gamma1, L1_gnn_beta1, L1_gnn_gamma2, L1_gnn_beta2, L1_gnn_W1, L1_gnn_b1, L1_gnn_W2, L1_gnn_b2)
    x = x + _L1_ffn_ref(_layernorm(x, axis=-1), L1_ffn_W_fx, L1_ffn_b_fx, L1_ffn_W_x, L1_ffn_b_x, L1_ffn_W_slice, L1_ffn_b_slice, L1_ffn_temperature, L1_ffn_hy_in_w, L1_ffn_hy_conv_w, L1_ffn_hy_conv_b, L1_ffn_hy_dt_bias, L1_ffn_hy_A_log, L1_ffn_hy_D, L1_ffn_hy_fcD_w, L1_ffn_hy_norm_w, L1_ffn_hy_out_w, L1_ffn_out_w, L1_ffn_out_b)
    return x

_drawn_inputs = setup_inputs


def setup_inputs(seed=0):
    import zlib

    import numpy as np

    out = dict(_drawn_inputs(seed))
    spreads = {'L1_ffn_b_fx': (0.0, 2.0),
     'L1_ffn_b_x': (0.0, 2.0),
     'L1_ffn_b_slice': (0.0, 2.0),
     'L1_ffn_temperature': (0.5, 0.6),
     'L1_ffn_hy_conv_b': (0.0, 2.0),
     'L1_ffn_hy_dt_bias': (-4.600166320800781, 0.6),
     'L1_ffn_hy_D': (1.0, 0.6),
     'L1_ffn_hy_norm_w': (1.0, 0.6),
     'L1_ffn_out_b': (0.0, 2.0)}
    factors = {'L0_ffn_Wq_pk': 8.0,
     'L0_ffn_pk_keys': 8.0,
     'L0_ffn_Wq': 29.048,
     'L0_ffn_keys_table': 28.149,
     'L0_ffn_values_table': 8.0,
     'L0_ffn_Wo': 8.0,
     'L1_gnn_gamma1': 7.457,
     'L1_gnn_beta1': 6.553,
     'L1_gnn_gamma2': 44.264,
     'L1_gnn_beta2': 41.777,
     'L1_gnn_W1': 3.136,
     'L1_gnn_b1': 64.0,
     'L1_gnn_W2': 3.064,
     'L1_gnn_b2': 55.869,
     'L1_ffn_W_fx': 17.475,
     'L1_ffn_W_x': 32.723,
     'L1_ffn_W_slice': 32.893,
     'L1_ffn_hy_conv_w': 33.201,
     'L1_ffn_hy_A_log': 64.0,
     'L1_ffn_hy_fcD_w': 64.0,
     'L1_ffn_hy_in_w': 3.402,
     'L1_ffn_hy_out_w': 3.309,
     'L1_ffn_out_w': 3.34}
    for name, (base, spread) in spreads.items():
        noise = np.random.default_rng([zlib.crc32(name.encode()), seed]).standard_normal(out[name].shape)
        drawn = base * np.exp(spread * noise) if base else spread * noise
        out[name] = jnp.asarray(drawn.astype(out[name].dtype))
    for name, factor in factors.items():
        out[name] = (out[name] * factor).astype(out[name].dtype)
    return out
```

```python
from contextlib import ExitStack

import concourse.bass as bass
from concourse import mybir

F32 = mybir.dt.float32
I32 = mybir.dt.int32
U32 = mybir.dt.uint32
ALU = mybir.AluOpType
ACT = mybir.ActivationFunctionType
AX = mybir.AxisListType

B, T, D = 64, 128, 128
HEADS, DK = 8, 64
KEYS, TOPK = 128, 16
ROW = 2 * D
NK_HEAD = KEYS * KEYS
GH, GD = 8, 16
FF = 4 * D // 128
SH, SL, SP_ = 8, 64, 64
DI = SH * SP_
NS = 64
KC = DI // 128
PROJ = 2 * DI + 2 * NS + 2 * SH
XBC, DT = DI, 2 * DI + 2 * NS
EPS = 1e-5
LOWEST = -3.4028235e38
MASKED = -3.0e38
NEG_INF = -9000000000000000.0
SLOPE = 0.2
TEMP_MIN = 1e-6
CLAMP = 80.0

RECTS = [(0, 1, 16), (1, 1, 8), (2, 2, 5), (4, 4, 3), (8, 8, 1)]
CAND = sum(r * c for _, r, c in RECTS)

GROUP = 4
GROUPS = TOPK // GROUP
RING = 8
G_LAG = 3
SLOTS = 2 * HEADS * GROUPS + G_LAG + 1
JUNK = 4

PARAMS = [
    ("a_cols", 4), ("wq", HEADS * D), ("wo", HEADS * D), ("gb_cols", 4), ("b1_cols", FF),
    ("g1_row", D), ("be1_row", D), ("b2_row", D), ("outb_row", D), ("w1", FF * 128), ("w2", FF * D),
    ("wfx", DI), ("bfx_row", DI), ("bslice_row", SL), ("temp_row", SH), ("inw", KC * PROJ),
    ("convw", 6 * 3), ("convb", 6), ("dtb_row", 2 * SH), ("alog_row", 2 * SH), ("fcd", KC * SH),
    ("dp_row", SH), ("normw", KC), ("hyout", KC * DI), ("outw", KC * D),
]
FACTORS = [("wqpk_t", 16 * D), ("keys_t", 16 * KEYS), ("wx", SH * D), ("bx", SH), ("wslice_t", SL)]


class Tiles:
    pass


def places(table):
    at, found = 0, {}
    for name, width in table:
        found[name] = (at, at + width)
        at += width
    return found, at


PARAM_AT, PARAM_COLS = places(PARAMS)
FACTOR_AT, FACTOR_COLS = places(FACTORS)

SIGNALS = """
load_done const_done fold_row fold_mm fold_out
vector_steps scalar_steps
hand_idx hand_w hand_h2T hand_kv hand_x3
a_x_in a_adj_in a_var a_rstd a_h a_hT_ps a_hT a_hTa a_scores a_alpha a_p a_pT_ps a_pT a_o a_h2
a_h2T_ps a_h2T a_sim_ps a_sims a_wdiff a_wexp
g_vec_used g_pe_used g_diag g_head_ps g_head
c_adj_in c_q_ps c_q c_k_ps c_k c_s_ps c_max c_p c_pn c_pT_ps c_pT c_o_ps c_o c_wo c_var c_rstd
c_n c_nT_ps c_nT c_qkv c_qm c_g_ps c_gsc c_gmax c_gp c_gpT_ps c_gpT c_go c_n2 c_n2T_ps c_y2T
c_hid_ps c_gelu c_mlp
d_var d_rstd d_u d_uT_ps d_uT d_l_ps d_z d_e d_fx_ps d_fx d_sw d_st_ps d_stn d_swT_ps d_swT
d_stT_ps d_stT d_z_ps d_x_ps d_dt_ps d_xp d_dta d_zc d_tap d_ln d_ez d_dtA d_xcl d_dA d_ex d_ed
d_xc d_DA_ps d_G_ps d_Gs d_M d_xn_ps d_fd_ps d_xn d_y_ps d_yg d_rr d_ygn d_ygT_ps d_ygT d_ot_ps
d_obd d_R_ps d_R d_f_ps d_out d_stored
""".split()


class Chain:

    def __init__(self, engine, semaphore):
        self.engine, self.semaphore, self.n = engine, semaphore, 0

    def ready(self):
        if self.n:
            self.engine.wait_ge(self.semaphore, self.n)

    def did(self, instruction):
        self.n += 1
        instruction.then_inc(self.semaphore, 1)


def over(ap, parts, rows, cols, dim):
    return ap.unsqueeze(dim).broadcast_to([parts, rows, cols])


def lay_out_memory(nc, ctx):
    def sb(name, shape, dtype=F32):
        return ctx.enter_context(nc.sbuf_tensor(name, shape, dtype))

    m = Tiles()
    m.params = sb("params_sb", [128, PARAM_COLS])
    m.p = {k: m.params[:, a:b] for k, (a, b) in PARAM_AT.items()}
    m.ring = sb("ring", [128, RING, GROUP, ROW])
    m.factors = m.ring[0:64].rearrange("p a b c -> p (a b c)")[:, 0:FACTOR_COLS]
    m.f = {k: m.factors[:, a:b] for k, (a, b) in FACTOR_AT.items()}
    m.wsim = sb("wsim", [128, 16 * KEYS])
    m.wslice = sb("wslice", [128, SH * SL])
    m.lbias = sb("lbias", [128, SH * SL])
    m.ea = sb("ea", [64, 2 * SH])
    m.invt = sb("invt", [128, SH])
    m.ident = sb("ident", [128, 128])
    m.causal = sb("causal", [128, 128])
    m.headmask = sb("headmask", [128, GH])
    m.identf = sb("identf", [64, 64])
    m.identb = sb("identb", [64, 64])
    m.identrep = sb("identrep", [64, SH, SL])
    m.ones = sb("ones", [64, 64])
    m.iota = sb("iota", [128, CAND])
    m.hoff = sb("hoff", [128, HEADS, TOPK])
    m.eps = sb("eps", [128, 1])
    m.one = sb("one", [128, 1])
    m.hand_a = sb("hand_a", [128, 2, 128])
    m.hand_g = sb("hand_g", [128, 2, 128])
    m.hand_c = sb("hand_c", [128, 2, 128])
    m.idx_a = sb("idx_a", [128, HEADS * TOPK], U32)
    m.idx_g = sb("idx_g", [128, HEADS * TOPK], U32)
    m.w_a = sb("w_a", [128, HEADS * TOPK])
    m.w_g = sb("w_g", [128, HEADS * TOPK])
    m.kv_g = sb("kv_g", [128, HEADS, ROW])
    m.kv_c = sb("kv_c", [128, HEADS, ROW])
    m.x3_c = sb("x3_c", [128, 128])
    m.x3_d = sb("x3_d", [128, 128])
    m.ax = sb("ax", [128, 128])
    m.aadj = sb("aadj", [128, 128], I32)
    m.ast = sb("ast", [128, 6])
    m.amv = sb("amv", [128, 2])
    m.arstd = sb("arstd", [128, 2])
    m.ah = sb("ah", [128, 128])
    m.ahT = sb("ahT", [128, 128])
    m.ahTa = sb("ahTa", [128, 4, 128])
    m.amask = sb("amask", [128, 4, 128], I32)
    m.alpha = sb("alpha", [128, 128])
    m.anm = sb("anm", [128, 4])
    m.ap = sb("ap", [128, 128])
    m.apT = sb("apT", [128, 128])
    m.sims = sb("sims", [128, 16, KEYS])
    m.top = sb("top", [128, 16, TOPK])
    m.topi = sb("topi", [128, 16, TOPK], U32)
    m.idxf = sb("idxf", [128, 2, HEADS, TOPK])
    m.cs = sb("cs", [128, HEADS, CAND])
    m.ci = sb("ci", [128, HEADS, CAND])
    m.fin = sb("fin", [128, HEADS, TOPK])
    m.pos = sb("pos", [128, TOPK], U32)
    m.posf = sb("posf", [128, TOPK])
    m.junk = sb("junk", [128, JUNK, CAND])
    m.chosen = sb("chosen", [128, HEADS, TOPK])
    m.wsum = sb("wsum", [128, HEADS])
    m.diag = sb("diag", [128, GROUP, 128])
    m.cadj = sb("cadj", [128, 128], I32)
    m.cbias = sb("cbias", [128, 128])
    m.cq = sb("cq", [128, HEADS, 128])
    m.ck = sb("ck", [128, HEADS, 128])
    m.catt = sb("catt", [128, HEADS, 128])
    m.cpT = sb("cpT", [128, HEADS, 128])
    m.coT = m.cq
    m.cnm = sb("cnm", [128, HEADS])
    m.csum = sb("csum", [128, HEADS])
    m.crs = sb("crs", [128, HEADS])
    m.cx2 = sb("cx2", [128, 128])
    m.cst = sb("cst", [128, 6])
    m.cmv = sb("cmv", [128, 2])
    m.crstd = sb("crstd", [128, 2])
    m.cy = sb("cy", [128, 128])
    m.cn = sb("cn", [128, 128])
    m.cnT = sb("cnT", [128, 128])
    m.cqkv = sb("cqkv", [128, 128])
    m.cqm = m.ck
    m.cxp = sb("cxp", [128, 128])
    m.cres = sb("cres", [128, 128])
    m.cy2T = sb("cy2T", [128, 128])
    m.cgT = sb("cgT", [128, FF, 128])
    m.dst6 = sb("dst6", [128, 6])
    m.dmv = sb("dmv", [128, 2])
    m.drstd = sb("drstd", [128, 2])
    m.du = sb("du", [128, 128])
    m.duT = sb("duT", [128, 128])
    m.dres = sb("dres", [128, 128])
    m.dz = sb("dz", [128, SH, SL])
    m.dnm = sb("dnm", [128, SH])
    m.dsw = sb("dsw", [128, SH, SL])
    m.dfx = sb("dfx", [128, SH, SP_ + 1])
    m.dden = sb("dden", [64, SH])
    m.dstn = sb("dstn", [64, SH, SP_])
    m.dswT = sb("dswT", [128, KC, 128])
    m.dstT = sb("dstT", [128, KC, 64])
    m.dxp = sb("dxp", [128, 6, SL + 2])
    m.dxc = sb("dxc", [128, 6, SL])
    m.dex = sb("dex", [128, 6, SL])
    m.ddt = sb("ddt", [64, 2 * SH])
    m.ddtm = sb("ddtm", [64, 2 * SH])
    m.ddta = sb("ddta", [64, 2 * SH])
    m.ddA = sb("ddA", [64, 2 * SH])
    m.dzc = sb("dzc", [64, DI])
    m.dsilz = m.dzc
    m.ded = sb("ded", [64, 2, SH, SL])
    m.dL = sb("dL", [64, 2, SH, SL])
    m.dG = sb("dG", [64, SL])
    m.dMf = sb("dMf", [64, SH, SL + 1])
    m.dMb = sb("dMb", [64, SH, SL + 1])
    m.dxn = sb("dxn", [64, SH, SP_])
    m.dfd = sb("dfd", [64, SH])
    m.dyg = sb("dyg", [64, SH, SP_])
    m.dsq = m.ded[:, 0, :, :].rearrange("p h t -> p (h t)")
    m.dss = sb("dss", [64, 2])
    m.dygT = sb("dygT", [128, KC, 64])
    m.dobd = sb("dobd", [128, KC, 128])
    m.dR = sb("dR", [128, KC, 128])
    m.dout = m.dres
    for_name = lambda name: ctx.enter_context(nc.psum_tensor(name, [128, 512], F32))
    m.A0, m.A1, m.G0 = for_name("A0"), for_name("A1"), for_name("G0")
    m.C0, m.C1 = for_name("C0"), for_name("C1")
    m.D0, m.D1, m.D2 = for_name("D0"), for_name("D1"), for_name("D2")
    return m


def heads4(bank, n=128):
    return bank[:, 0:4 * n].rearrange("p (h n) -> p h n", h=4)


def set_up(nc, m, s, params, factors):
    with nc.Block(no_gpsimd_drain=True) as block:

        @block.sync
        def _(sp):
            sp.dma_start(m.factors, factors).then_inc(s["load_done"], 16)
            sp.dma_start(m.params[:, :], params).then_inc(s["load_done"], 16)

        @block.gpsimd
        def _(pool):
            def const(instruction, n=[0]):
                n[0] += 1
                instruction.then_inc(s["const_done"], 1)
                pool.wait_ge(s["const_done"], n[0])

            const(pool.memset(m.ident[:, :], 0.0))
            const(pool.affine_select(out=m.ident[:, :], in_=m.ident[:, :], compare_op=ALU.not_equal, fill=1.0,
                                     base=0, pattern=[[-1, 128]], channel_multiplier=1))
            const(pool.memset(m.causal[:, :], 0.0))
            const(pool.affine_select(out=m.causal[:, :], in_=m.causal[:, :], compare_op=ALU.is_ge, fill=MASKED,
                                     base=0, pattern=[[-1, 128]], channel_multiplier=1))
            const(pool.memset(m.headmask[:, :], 1.0))
            const(pool.affine_select(out=m.headmask[:, :], in_=m.headmask[:, :], compare_op=ALU.is_ge, fill=0.0,
                                     base=0, pattern=[[-GD, GH]], channel_multiplier=1))
            const(pool.affine_select(out=m.headmask[:, :], in_=m.headmask[:, :], compare_op=ALU.is_ge, fill=0.0,
                                     base=GD - 1, pattern=[[GD, GH]], channel_multiplier=-1))
            const(pool.iota(m.iota[:, :], pattern=[[1, CAND]], base=0, channel_multiplier=0,
                            allow_small_or_imprecise_dtypes=True))
            const(pool.iota(m.hoff[:, :, :], pattern=[[NK_HEAD, HEADS], [0, TOPK]], base=0, channel_multiplier=0,
                            allow_small_or_imprecise_dtypes=True))
            for tile in (m.dMf, m.dMb, m.dxp, m.dobd):
                const(pool.memset(tile[:, :, :], 0.0))
            const(pool.memset(m.dfx[:, :, :], 1.0))
            const(pool.memset(m.dxc[:, :, :], 0.0))

        @block.scalar
        def _(act):
            act.wait_ge(s["load_done"], 32)
            act.wait_ge(s["fold_mm"], 1)
            for c, bank in enumerate((m.A0, m.A1, m.C0, m.C1)):
                act.activation(m.wsim[:, 512 * c:512 * (c + 1)], bank[:, :], ACT.Copy).then_inc(s["scalar_steps"], 1)
            act.wait_ge(s["fold_row"], 1)
            act.activation(m.ea[:, :], m.ea[:, :], ACT.Exp).then_inc(s["scalar_steps"], 1)

        @block.tensor
        def _(pe):
            pe.wait_ge(s["load_done"], 32)
            for i in range(16):
                bank = (m.A0, m.A1, m.C0, m.C1)[i // 4]
                pe.matmul(bank[:, 128 * (i % 4):128 * (i % 4 + 1)], m.f["wqpk_t"][:, 128 * i:128 * (i + 1)],
                          m.f["keys_t"][:, 128 * i:128 * (i + 1)], start=True, stop=True)
            for h in range(SH):
                last = pe.matmul(m.D0[:, SL * h:SL * (h + 1)], m.f["wx"][:, D * h:D * (h + 1)], m.f["wslice_t"],
                                 start=True, stop=True)
            last.then_inc(s["fold_mm"], 1)
            pe.wait_ge(s["fold_out"], 1)
            for h in range(SH):
                last = pe.matmul(m.D1[:, SL * h:SL * (h + 1)], m.sims[0:64, h, :], m.f["wslice_t"],
                                 start=True, stop=True)
            last.then_inc(s["fold_mm"], 1)

        @block.vector
        def _(dve):
            chain = Chain(dve, s["vector_steps"])

            def step(instruction):
                chain.did(instruction)
                chain.ready()

            dve.wait_ge(s["load_done"], 32)
            dve.tensor_scalar(m.ea[:, :], m.p["alog_row"][0:64], CLAMP, None, ALU.min).then_inc(s["fold_row"], 1)
            dve.tensor_copy(m.sims[0:64, 0:SH, :], over(m.f["bx"], 64, SH, 128, 2)).then_inc(s["fold_out"], 1)
            step(dve.memset(m.eps[:, :], EPS))
            step(dve.memset(m.one[:, :], 1.0))
            step(dve.memset(m.ones[:, :], 1.0))
            step(dve.tensor_scalar(m.invt[:, :], m.p["temp_row"], TEMP_MIN, None, ALU.max))
            step(dve.reciprocal(m.invt[:, :], m.invt[:, :]))
            for k in range(KC):
                cols = m.p["hyout"][:, DI * k:DI * (k + 1)]
                step(dve.tensor_scalar(cols, cols, m.p["normw"][:, k:k + 1], None, ALU.mult))
            dve.wait_ge(s["const_done"], 2)
            step(dve.tensor_copy(m.identf[:, :], m.ident[0:64, 0:64]))
            step(dve.tensor_copy(m.identb[:, :], m.ident[0:64, 0:64]))
            step(dve.memset(m.identf[:, 0:1], 0.0))
            step(dve.memset(m.identb[:, SL - 1:SL], 0.0))
            step(dve.tensor_copy(m.identrep[:, :, :], over(m.ident[0:64, 0:64], 64, SH, SL, 1)))
            by_head = over(m.invt[:, :], 128, SH, SL, 2)
            dve.wait_ge(s["fold_mm"], 2)
            wslice = m.wslice[:, :].rearrange("p (h g) -> p h g", h=SH)
            lbias = m.lbias[:, :].rearrange("p (h g) -> p h g", h=SH)
            step(dve.tensor_tensor(wslice, m.D0[:, :].rearrange("p (h g) -> p h g", h=SH), by_head, ALU.mult))
            step(dve.tensor_tensor(lbias, m.D1[:, :].rearrange("p (h g) -> p h g", h=SH),
                                   over(m.p["bslice_row"], 128, SH, SL, 1), ALU.add))
            step(dve.tensor_tensor(lbias, lbias, by_head, ALU.mult))


def turn(nc, m, s, dram, a=None, g=None, c=None, d=None):
    do_a, do_g, do_c, do_d = a is not None, g is not None, c is not None, d is not None
    p = m.p

    def gathered_by(n):
        per_turn = HEADS * GROUPS // RING
        return (g * per_turn + n // RING + 1) * (16 * GROUP)

    c_at = {(5 * k) // 2: k for k in range(26)}
    d_at = {(7 * k) // 2 + 1: k for k in range(18)}

    with nc.Block(no_gpsimd_drain=True) as block:

        @block.sync
        def _(sp):
            if do_a:
                sp.dma_start(m.ax[:, :], dram["x"][a]).then_inc(s["a_x_in"], 16)
                sp.dma_start(m.aadj[:, :], dram["adj"][a]).then_inc(s["a_adj_in"], 16)
            if do_c:
                sp.dma_start(m.cadj[:, :], dram["adj"][c]).then_inc(s["c_adj_in"], 16)
            if do_d:
                sp.wait_ge(s["d_out"], 1)
                sp.dma_start(dram["out"][d], m.dout[:, :]).then_inc(s["d_stored"], 16)
                sp.wait_ge(s["d_stored"], 16)

        @block.gpsimd
        def _(pool):
            if not do_g:
                return
            pool.wait_ge(s["hand_idx"], 1)
            for n in range(HEADS * GROUPS):
                h, r = divmod(n, GROUPS)
                if n >= RING:
                    pool.wait_ge(s["g_pe_used"] if h % 2 else s["g_vec_used"], (h // 2 - 1) * GROUPS + r + 1)
                for k in range(GROUP):
                    i = h * TOPK + r * GROUP + k
                    pool.indirect_dma_start(
                        out=m.ring[:, n % RING, k, :], out_offset=None, in_=dram["table"],
                        in_offset=bass.IndirectOffsetOnAxis(ap=m.idx_g[:, i:i + 1], axis=0),
                    ).then_inc(s["gathered"][n % RING], 16)

        @block.tensor
        def _(pe):
            def transpose(out, in_, n):
                return pe.transpose(out, in_, m.ident[0:n, 0:n])

            def stage_a(slot):
                if slot == 2:
                    pe.wait_ge(s["a_h"], 1)
                    transpose(m.A0[:, 0:128], m.ah[:, :], 128).then_inc(s["a_hT_ps"], 1)
                if slot == 3:
                    pe.wait_ge(s["a_hTa"], 1)
                    pe.matmul(m.A1[:, :], m.ahT[:, :], m.ahTa[:, :, :], start=True, stop=True).then_inc(s["a_scores"], 1)
                if slot == 5:
                    pe.wait_ge(s["a_p"], 1)
                    transpose(m.A0[:, 0:128], m.ap[:, :], 128).then_inc(s["a_pT_ps"], 1)
                if slot == 6:
                    pe.wait_ge(s["a_pT"], 1)
                    pe.matmul(m.A1[:, 0:128], m.apT[:, :], m.ah[:, :], start=True, stop=True).then_inc(s["a_o"], 1)
                if slot == 8:
                    pe.wait_ge(s["a_h2"], 1)
                    transpose(m.A0[:, 0:128], m.ah[:, :], 128).then_inc(s["a_h2T_ps"], 1)
                if 9 <= slot < 13:
                    k = slot - 9
                    pe.wait_ge(s["a_h2T"], 1)
                    if k >= 2:
                        pe.wait_ge(s["a_sims"], k - 1)
                    pe.matmul((m.A1, m.A0)[k % 2][:, :], m.hand_a[:, 1, :], m.wsim[:, 512 * k:512 * (k + 1)],
                              start=True, stop=True).then_inc(s["a_sim_ps"], 1)

            def stage_g(slot):
                n, second = divmod(slot - G_LAG, 2)
                if second or not 0 <= n < HEADS * GROUPS or n // GROUPS % 2 == 0:
                    return
                h, r = divmod(n, GROUPS)
                turn_of_pe = (h // 2) * GROUPS + r
                pe.wait_ge(s["gathered"][n % RING], gathered_by(n))
                pe.wait_ge(s["g_diag"], turn_of_pe + 1)
                if r == 0 and h > 1:
                    pe.wait_ge(s["g_head"], h // 2)
                for k in range(GROUP):
                    last = pe.matmul(m.G0[:, 0:ROW], m.diag[:, k, :], m.ring[:, n % RING, k, :],
                                     start=(r == 0 and k == 0), stop=(r == GROUPS - 1 and k == GROUP - 1))
                last.then_inc(s["g_pe_used"], 1)

            def stage_c(k):
                if k in (1, 2):
                    half = k - 1
                    pe.wait_ge(s["hand_h2T"], 1)
                    bank = heads4((m.C0, m.C1)[half])
                    for j in range(4):
                        h = 4 * half + j
                        last = pe.matmul(bank[:, j, :], p["wq"][:, D * h:D * (h + 1)], m.hand_c[:, 1, :],
                                         start=True, stop=True)
                    last.then_inc(s["c_q_ps"], 1)
                if k in (3, 4):
                    half = k - 3
                    pe.wait_ge(s["hand_kv"], 1)
                    pe.wait_ge(s["c_q"], half + 1)
                    bank = heads4((m.C0, m.C1)[half])
                    for j in range(4):
                        last = transpose(bank[:, j, :], m.kv_c[:, 4 * half + j, 0:D], 128)
                    last.then_inc(s["c_k_ps"], 1)
                if k in (5, 6):
                    half = k - 5
                    pe.wait_ge(s["c_k"], half + 1)
                    bank = heads4((m.C0, m.C1)[half])
                    for j in range(4):
                        h = 4 * half + j
                        last = pe.matmul(bank[:, j, :], m.cq[:, h, :], m.ck[:, h, :], start=True, stop=True)
                    last.then_inc(s["c_s_ps"], 1)
                if k in (8, 9):
                    half = k - 8
                    pe.wait_ge(s["c_pn"], 1)
                    bank = heads4((m.C0, m.C1)[half])
                    for j in range(4):
                        last = transpose(bank[:, j, :], m.catt[:, 4 * half + j, :], 128)
                    last.then_inc(s["c_pT_ps"], 1)
                if k in (10, 11):
                    half = k - 10
                    pe.wait_ge(s["c_pT"], half + 1)
                    bank = heads4((m.C0, m.C1)[half])
                    for j in range(4):
                        h = 4 * half + j
                        last = pe.matmul(bank[:, j, :], m.kv_c[:, h, D:ROW], m.cpT[:, h, :], start=True, stop=True)
                    last.then_inc(s["c_o_ps"], 1)
                if k == 12:
                    pe.wait_ge(s["c_o"], 2)
                    for h in range(HEADS):
                        last = pe.matmul(m.C0[:, 0:D], m.coT[:, h, :], p["wo"][:, D * h:D * (h + 1)],
                                         start=(h == 0), stop=(h == HEADS - 1))
                    last.then_inc(s["c_wo"], 1)
                if k == 15:
                    pe.wait_ge(s["c_n"], 1)
                    transpose(m.C1[:, 0:128], m.cn[:, :], 128).then_inc(s["c_nT_ps"], 1)
                if k in (16, 17):
                    half = k - 16
                    pe.wait_ge(s["c_qm"], 1)
                    pe.matmul((m.C0, m.C1)[half][:, :], m.cnT[:, :], m.cqm[:, 4 * half:4 * half + 4, :],
                              start=True, stop=True).then_inc(s["c_g_ps"], 1)
                if k in (19, 20):
                    half = k - 19
                    pe.wait_ge(s["c_gp"], 1)
                    bank = heads4((m.C0, m.C1)[half])
                    for j in range(4):
                        last = transpose(bank[:, j, :], m.catt[:, 4 * half + j, :], 128)
                    last.then_inc(s["c_gpT_ps"], 1)
                if k == 21:
                    pe.wait_ge(s["c_gpT"], 2)
                    pe.wait_ge(s["c_qkv"], 1)
                    for h in range(GH):
                        cols = slice(GD * h, GD * (h + 1))
                        last = pe.matmul(m.C0[:, cols], m.cpT[:, h, :], m.cqkv[:, cols], start=True, stop=True)
                    last.then_inc(s["c_go"], 1)
                if k == 23:
                    pe.wait_ge(s["c_n2"], 1)
                    transpose(m.C1[:, 0:128], m.cn[:, :], 128).then_inc(s["c_n2T_ps"], 1)
                if k == 24:
                    pe.wait_ge(s["c_y2T"], 1)
                    for f in range(FF):
                        last = pe.matmul(m.C0[:, 128 * f:128 * (f + 1)], p["w1"][:, 128 * f:128 * (f + 1)],
                                         m.cy2T[:, :], start=True, stop=True)
                    last.then_inc(s["c_hid_ps"], 1)
                if k == 25:
                    pe.wait_ge(s["c_gelu"], 1)
                    for f in range(FF):
                        last = pe.matmul(m.C1[:, 0:D], m.cgT[:, f, :], p["w2"][:, D * f:D * (f + 1)],
                                         start=(f == 0), stop=(f == FF - 1))
                    last.then_inc(s["c_mlp"], 1)

            def stage_d(k):
                inw = p["inw"].rearrange("p (k n) -> p k n", k=KC)
                if k == 2:
                    pe.wait_ge(s["d_u"], 1)
                    transpose(m.D0[:, 0:128], m.du[:, :], 128).then_inc(s["d_uT_ps"], 1)
                if k == 3:
                    pe.wait_ge(s["d_uT"], 1)
                    pe.matmul(m.D1[:, :], m.duT[:, :], m.wslice[:, :], start=True, stop=True).then_inc(s["d_l_ps"], 1)
                if k == 4:
                    pe.matmul(m.D0[:, :], m.duT[:, :], p["wfx"], start=True, stop=True).then_inc(s["d_fx_ps"], 1)
                if k == 5:
                    pe.wait_ge(s["d_sw"], 1)
                    for h in range(SH):
                        cols = slice((SP_ + 1) * (h % 4), (SP_ + 1) * (h % 4 + 1))
                        last = pe.matmul((m.D0, m.D1)[h // 4][0:64, cols], m.dsw[:, h, :], m.dfx[:, h, :],
                                         start=True, stop=True)
                    last.then_inc(s["d_st_ps"], 1)
                if k == 6:
                    for j in range(KC):
                        last = transpose(m.D2[:, 128 * j:128 * (j + 1)],
                                         m.dsw[:, 2 * j:2 * j + 2, :].rearrange("p a b -> p (a b)"), 128)
                    last.then_inc(s["d_swT_ps"], 1)
                    pe.wait_ge(s["d_stn"], 1)
                    for j in range(KC):
                        last = transpose(m.D0[:, 64 * j:64 * (j + 1)],
                                         m.dstn[:, 2 * j:2 * j + 2, :].rearrange("p a b -> p (a b)"), 64)
                    last.then_inc(s["d_stT_ps"], 1)
                if k == 7:
                    pe.wait_ge(s["d_stT"], 1)
                    pe.wait_ge(s["d_swT"], 1)
                    for j in range(KC):
                        last = pe.matmul(m.D2[0:64, :], m.dstT[:, j, :], inw[:, j, 0:DI],
                                         start=(j == 0), stop=(j == KC - 1))
                    last.then_inc(s["d_z_ps"], 1)
                    for j in range(KC):
                        last = pe.matmul(m.D0[0:64, 0:2 * SH], m.dstT[:, j, :], inw[:, j, DT:PROJ],
                                         start=(j == 0), stop=(j == KC - 1))
                    last.then_inc(s["d_dt_ps"], 1)
                    for q in range(6):
                        first = XBC + 128 * min(q, 4) + 64 * (q == 5)
                        rows = 128 if q < 4 else 64
                        for j in range(KC):
                            last = pe.matmul(m.D1[0:rows, 64 * q:64 * (q + 1)], inw[:, j, first:first + rows],
                                             m.dstT[:, j, :], start=(j == 0), stop=(j == KC - 1))
                    last.then_inc(s["d_x_ps"], 1)
                if k == 10:
                    pe.wait_ge(s["d_ed"], 1)
                    pe.matmul(m.D1[0:64, :], m.ones[:, :], m.ded[:, 0, :, :], start=True, stop=True)
                    pe.matmul(m.D2[0:64, :], m.ones[:, :], m.ded[:, 1, :, :], start=True, stop=True)\
                        .then_inc(s["d_DA_ps"], 1)
                    pe.wait_ge(s["d_xc"], 1)
                    pe.matmul(m.D0[0:64, 0:SL], m.dxc[0:64, 4, :], m.dxc[0:64, 5, :], start=True, stop=True)\
                        .then_inc(s["d_G_ps"], 1)
                if k == 11:
                    pe.wait_ge(s["d_Gs"], 1)
                    fcd = p["fcd"].rearrange("p (k n) -> p k n", k=KC)
                    for j in range(KC):
                        last = pe.matmul(m.D0[0:64, 0:SH], m.dxc[:, j, :], fcd[:, j, :],
                                         start=(j == 0), stop=(j == KC - 1))
                    last.then_inc(s["d_fd_ps"], 1)
                    pe.wait_ge(s["d_M"], 1)
                    for j in range(KC):
                        last = transpose(m.D1[0:64, 128 * j:128 * (j + 1)], m.dxc[:, j, :], 128)
                    last.then_inc(s["d_xn_ps"], 1)
                if k == 12:
                    pe.wait_ge(s["d_xn"], 1)
                    for h in range(SH):
                        cols = slice(SP_ * h, SP_ * (h + 1))
                        pe.matmul(m.D2[0:64, cols], m.dMf[:, h, 0:SL], m.dxn[:, h, :], start=True, stop=False)
                        last = pe.matmul(m.D2[0:64, cols], m.dMb[:, h, 1:SL + 1], m.dxn[:, h, :],
                                         start=False, stop=True)
                    last.then_inc(s["d_y_ps"], 1)
                if k == 14:
                    pe.wait_ge(s["d_ygn"], 1)
                    for j in range(KC):
                        last = transpose(m.D0[:, 64 * j:64 * (j + 1)],
                                         m.dyg[:, 2 * j:2 * j + 2, :].rearrange("p a b -> p (a b)"), 64)
                    last.then_inc(s["d_ygT_ps"], 1)
                if k == 15:
                    pe.wait_ge(s["d_ygT"], 1)
                    hyout = p["hyout"].rearrange("p (k n) -> p k n", k=KC)
                    for q in range(KC):
                        for j in range(KC):
                            last = pe.matmul(m.D1[:, 64 * q:64 * (q + 1)], hyout[:, j, 128 * q:128 * (q + 1)],
                                             m.dygT[:, j, :], start=(j == 0), stop=(j == KC - 1))
                    last.then_inc(s["d_ot_ps"], 1)
                if k == 16:
                    pe.wait_ge(s["d_obd"], 1)
                    for q in range(KC):
                        last = pe.matmul(m.D2[:, 128 * q:128 * (q + 1)], m.dobd[:, q, :],
                                         p["outw"][:, D * q:D * (q + 1)], start=True, stop=True)
                    last.then_inc(s["d_R_ps"], 1)
                if k == 17:
                    pe.wait_ge(s["d_R"], 1)
                    for q in range(KC):
                        last = pe.matmul(m.D0[:, 0:D], m.dswT[:, q, :], m.dR[:, q, :],
                                         start=(q == 0), stop=(q == KC - 1))
                    last.then_inc(s["d_f_ps"], 1)

            for slot in range(SLOTS):
                if do_a:
                    stage_a(slot)
                if do_c and slot in c_at:
                    stage_c(c_at[slot])
                if do_d and slot in d_at:
                    stage_d(d_at[slot])
                if do_g:
                    stage_g(slot)

        @block.scalar
        def _(act):
            steps = Chain(act, s["scalar_steps"])

            def copy(out, in_):
                return act.activation(out, in_, ACT.Copy)

            def rstd(out, mv, ready):
                steps.did(act.activation(out[:, 0:1], mv[:, 1:2], ACT.Ln, bias=m.eps[:, :]))
                steps.ready()
                act.activation(out[:, 1:2], out[:, 0:1], ACT.Exp, scale=-0.5).then_inc(ready, 1)

            def stage_a(slot):
                if slot == 1:
                    act.wait_ge(s["a_var"], 1)
                    rstd(m.arstd, m.amv, s["a_rstd"])
                if slot == 2:
                    act.wait_ge(s["a_hT_ps"], 1)
                    copy(m.ahT[:, :], m.A0[:, 0:128]).then_inc(s["a_hT"], 1)
                if slot == 4:
                    act.wait_ge(s["a_alpha"], 1)
                    act.activation(m.ap[:, :], m.alpha[:, :], ACT.Exp, bias=m.anm[:, 0:1],
                                   accum_out=m.anm[:, 1:2]).then_inc(s["a_p"], 1)
                if slot == 5:
                    act.wait_ge(s["a_pT_ps"], 1)
                    copy(m.apT[:, :], m.A0[:, 0:128]).then_inc(s["a_pT"], 1)
                if slot == 7:
                    act.wait_ge(s["a_var"], 2)
                    rstd(m.arstd, m.amv, s["a_rstd"])
                if slot == 8:
                    act.wait_ge(s["a_h2T_ps"], 1)
                    copy(m.hand_a[:, 1, :], m.A0[:, 0:128]).then_inc(s["a_h2T"], 1)
                if 9 <= slot < 13:
                    k = slot - 9
                    act.wait_ge(s["a_sim_ps"], k + 1)
                    copy(m.sims[:, 4 * k:4 * k + 4, :], heads4((m.A1, m.A0)[k % 2])).then_inc(s["a_sims"], 1)
                if slot == 61:
                    act.wait_ge(s["a_wdiff"], 1)
                    act.activation(m.fin[:, :, :], m.fin[:, :, :], ACT.Exp).then_inc(s["a_wexp"], 1)

            def stage_g(slot):
                n, second = divmod(slot - G_LAG, 2)
                if not 0 <= n < HEADS * GROUPS or n // GROUPS % 2 == 0:
                    return
                h, r = divmod(n, GROUPS)
                turn_of_pe = (h // 2) * GROUPS + r
                if not second:
                    if turn_of_pe == 0:
                        act.wait_ge(s["hand_w"], 1)
                    else:
                        act.wait_ge(s["g_pe_used"], turn_of_pe)
                    for k in range(GROUP):
                        i = h * TOPK + r * GROUP + k
                        last = act.activation(m.diag[:, k, :], m.ident[:, :], ACT.Copy, scale=m.w_g[:, i:i + 1])
                    last.then_inc(s["g_diag"], 1)
                elif r == GROUPS - 1:
                    act.wait_ge(s["g_pe_used"], turn_of_pe + 1)
                    if h == 1 and do_c:
                        act.wait_ge(s["hand_kv"], 1)
                    copy(m.kv_g[:, h, :], m.G0[:, 0:ROW]).then_inc(s["g_head"], 1)

            def exps(scale_steps, ready):
                for h in range(HEADS):
                    last = act.activation(m.catt[:, h, :], m.catt[:, h, :], ACT.Exp, bias=m.cnm[:, h:h + 1],
                                          accum_out=m.csum[:, h:h + 1])
                last.then_inc(ready, 1)

            def stage_c(k):
                for first, at, ready, out in ((1, s["c_q_ps"], s["c_q"], m.cq), (3, s["c_k_ps"], s["c_k"], m.ck),
                                              (8, s["c_pT_ps"], s["c_pT"], m.cpT), (10, s["c_o_ps"], s["c_o"], m.coT),
                                              (19, s["c_gpT_ps"], s["c_gpT"], m.cpT)):
                    if k in (first, first + 1):
                        half = k - first
                        act.wait_ge(at, half + 1)
                        copy(out[:, 4 * half:4 * half + 4, :], heads4((m.C0, m.C1)[half])).then_inc(ready, 1)
                if k == 7:
                    act.wait_ge(s["c_max"], 1)
                    exps(1, s["c_p"])
                if k in (13, 14):
                    act.wait_ge(s["c_var"], k - 12)
                    rstd(m.crstd, m.cmv, s["c_rstd"])
                if k == 15:
                    act.wait_ge(s["c_nT_ps"], 1)
                    act.activation(m.cnT[:, :], m.C1[:, 0:128], ACT.Identity, bias=p["gb_cols"][:, 1:2],
                                   scale=p["gb_cols"][:, 0:1]).then_inc(s["c_nT"], 1)
                if k == 18:
                    act.wait_ge(s["c_gmax"], 1)
                    exps(1, s["c_gp"])
                if k == 22:
                    act.wait_ge(s["c_var"], 3)
                    rstd(m.crstd, m.cmv, s["c_rstd"])
                if k == 23:
                    act.wait_ge(s["c_n2T_ps"], 1)
                    act.activation(m.cy2T[:, :], m.C1[:, 0:128], ACT.Identity, bias=p["gb_cols"][:, 3:4],
                                   scale=p["gb_cols"][:, 2:3]).then_inc(s["c_y2T"], 1)
                if k == 24:
                    act.wait_ge(s["c_hid_ps"], 1)
                    for f in range(FF):
                        last = act.activation(m.cgT[:, f, :], m.C0[:, 128 * f:128 * (f + 1)], ACT.Gelu,
                                              bias=p["b1_cols"][:, f:f + 1])
                    last.then_inc(s["c_gelu"], 1)

            def stage_d(k):
                if k == 1:
                    act.wait_ge(s["d_var"], 1)
                    rstd(m.drstd, m.dmv, s["d_rstd"])
                if k == 2:
                    act.wait_ge(s["d_uT_ps"], 1)
                    copy(m.duT[:, :], m.D0[:, 0:128]).then_inc(s["d_uT"], 1)
                if k == 4:
                    act.wait_ge(s["d_z"], 1)
                    act.activation(m.dsw[:, :, :], m.dz[:, :, :], ACT.Exp).then_inc(s["d_e"], 1)
                if k == 6:
                    act.wait_ge(s["d_swT_ps"], 1)
                    copy(m.dswT[:, :, :], heads4(m.D2)).then_inc(s["d_swT"], 1)
                    act.wait_ge(s["d_stT_ps"], 1)
                    copy(m.dstT[:, :, :], heads4(m.D0, 64)).then_inc(s["d_stT"], 1)
                if k == 7:
                    act.wait_ge(s["d_x_ps"], 1)
                    copy(m.dxp[:, 0:4, 2:SL + 2], heads4(m.D1, 64))
                    copy(m.dxp[0:64, 4:6, 2:SL + 2], m.D1[0:64, 256:384].rearrange("p (a b) -> p a b", a=2))\
                        .then_inc(s["d_xp"], 1)
                if k == 8:
                    act.wait_ge(s["d_dta"], 1)
                    steps.did(act.activation(m.ddta[:, :], m.ddta[:, :], ACT.Exp))
                    steps.ready()
                    act.activation(m.ddta[:, :], m.ddta[:, :], ACT.Ln, bias=m.one[0:64, :]).then_inc(s["d_ln"], 1)
                    act.wait_ge(s["d_xp"], 1)
                    for q in range(6):
                        rows = 128 if q < 4 else 64
                        last = act.activation(m.dxc[0:rows, q, :], m.dxp[0:rows, q, 2:SL + 2], ACT.Identity,
                                              bias=p["convb"][0:rows, q:q + 1],
                                              scale=p["convw"][0:rows, 3 * q + 2:3 * q + 3])
                    last.then_inc(s["d_tap"], 1)
                    act.wait_ge(s["d_zc"], 1)
                    act.activation(m.dzc[:, :], m.dzc[:, :], ACT.Exp, scale=-1.0).then_inc(s["d_ez"], 1)
                if k == 9:
                    act.wait_ge(s["d_dtA"], 1)
                    act.activation(m.ddA[:, :], m.ddA[:, :], ACT.Exp, scale=-1.0).then_inc(s["d_dA"], 1)
                    act.wait_ge(s["d_xcl"], 1)
                    act.activation(m.dex[:, :, :], m.dex[:, :, :], ACT.Exp, scale=-1.0).then_inc(s["d_ex"], 1)
                if k == 10:
                    act.wait_ge(s["d_G_ps"], 1)
                    copy(m.dG[:, :], m.D0[0:64, 0:SL]).then_inc(s["d_Gs"], 1)
                if k == 11:
                    act.wait_ge(s["d_xn_ps"], 1)
                    copy(m.dxn[:, :, :], m.D1[0:64, :].rearrange("p (h c) -> p h c", h=SH)).then_inc(s["d_xn"], 1)
                if k == 13:
                    act.wait_ge(s["d_yg"], 1)
                    steps.did(act.activation(m.dsq, m.dyg[:, :, :].rearrange("p h c -> p (h c)"), ACT.Square,
                                             accum_out=m.dss[:, 0:1]))
                    steps.ready()
                    steps.did(act.activation(m.dss[:, 1:2], m.dss[:, 0:1], ACT.Ln, bias=m.eps[0:64, :],
                                             scale=1.0 / DI))
                    steps.ready()
                    act.activation(m.dss[:, 0:1], m.dss[:, 1:2], ACT.Exp, scale=-0.5).then_inc(s["d_rr"], 1)
                if k == 14:
                    act.wait_ge(s["d_ygT_ps"], 1)
                    copy(m.dygT[:, :, :], heads4(m.D0, 64)).then_inc(s["d_ygT"], 1)
                if k == 15:
                    act.wait_ge(s["d_ot_ps"], 1)
                    copy(m.dobd[0:64, :, 0:64], m.D1[0:64, 0:256].rearrange("p (q g) -> p q g", q=KC))
                    copy(m.dobd[64:128, :, 64:128], m.D1[64:128, 0:256].rearrange("p (q g) -> p q g", q=KC))\
                        .then_inc(s["d_obd"], 1)
                if k == 16:
                    act.wait_ge(s["d_R_ps"], 1)
                    copy(m.dR[:, :, :], heads4(m.D2)).then_inc(s["d_R"], 1)

            if do_c:
                copy(m.kv_c[:, :, :], m.kv_g[:, :, :]).then_inc(s["hand_kv"], 1)
            for slot in range(SLOTS):
                if do_a:
                    stage_a(slot)
                if do_c and slot in c_at:
                    stage_c(c_at[slot])
                if do_d and slot in d_at:
                    stage_d(d_at[slot])
                if do_g:
                    stage_g(slot)

        @block.vector
        def _(dve):
            chain = Chain(dve, s["vector_steps"])

            def step(instruction):
                chain.did(instruction)
                chain.ready()

            def moments(x, stats, mv, ready):
                step(dve.bn_stats(stats, x))
                dve.bn_aggr(mv, stats).then_inc(ready, 1)

            def normalize(out, x, mv, rstd):
                return dve.tensor_scalar(out, x, mv[:, 0:1], rstd[:, 1:2], ALU.subtract, ALU.mult)

            def top16(values, n_index, scores):
                step(dve.max(values[:, 0:8], scores))
                step(dve.max_index(n_index[:, 0:8], values[:, 0:8], scores))
                step(dve.match_replace(scores, values[:, 0:8], scores, LOWEST))
                step(dve.max(values[:, 8:16], scores))
                step(dve.max_index(n_index[:, 8:16], values[:, 8:16], scores))

            def pairs(out, first, second, h0, h1):
                at = 0
                for i0, rows, cols in RECTS:
                    o = out[:, :, at:at + rows * cols].rearrange("p h (i j) -> p h i j", i=rows)
                    x = first[:, :, i0:i0 + rows].unsqueeze(3).broadcast_to([128, HEADS, rows, cols])
                    y = second[:, :, 0:cols].unsqueeze(2).broadcast_to([128, HEADS, rows, cols])
                    if rows == 1:
                        o, x, y = o[:, :, 0, :], x[:, :, 0, :], y[:, :, 0, :]
                    if cols == 1:
                        o, x, y = o[:, :, :, 0], x[:, :, :, 0], y[:, :, :, 0]
                    step(dve.tensor_tensor(o, x, y, ALU.add))
                    at += rows * cols

            def stage_a(slot):
                if slot == 0:
                    dve.wait_ge(s["a_x_in"], 16)
                    moments(m.ax[:, :], m.ast[:, :], m.amv[:, :], s["a_var"])
                if slot == 1:
                    dve.wait_ge(s["a_rstd"], 1)
                    normalize(m.ah[:, :], m.ax[:, :], m.amv, m.arstd).then_inc(s["a_h"], 1)
                    dve.wait_ge(s["a_adj_in"], 16)
                    for k in range(4):
                        dve.tensor_scalar(m.amask[:, k, :], m.aadj[:, :], float(k + 1), None, ALU.is_equal)
                    step(dve.memset(m.alpha[:, :], NEG_INF / SLOPE))
                if slot == 2:
                    dve.wait_ge(s["a_hT"], 1)
                    for k in range(4):
                        last = dve.tensor_scalar(m.ahTa[:, k, :], m.ahT[:, :], p["a_cols"][:, k:k + 1], None, ALU.mult)
                    last.then_inc(s["a_hTa"], 1)
                if slot == 3:
                    dve.wait_ge(s["a_scores"], 1)
                    for k in range(4):
                        step(dve.copy_predicated(m.alpha[:, :], m.amask[:, k, :], m.A1[:, 128 * k:128 * (k + 1)]))
                    step(dve.scalar_tensor_tensor(out=m.alpha[:, :], in0=m.alpha[:, :], scalar=SLOPE,
                                                  in1=m.alpha[:, :], op0=ALU.mult, op1=ALU.max))
                    dve.tensor_reduce(m.anm[:, 0:1], m.alpha[:, :], AX.X, ALU.max, negate=True).then_inc(s["a_alpha"], 1)
                if slot == 4:
                    dve.wait_ge(s["a_p"], 1)
                    step(dve.reciprocal(m.anm[:, 2:3], m.anm[:, 1:2]))
                if slot == 6:
                    dve.wait_ge(s["a_o"], 1)
                    step(dve.scalar_tensor_tensor(out=m.hand_a[:, 0, :], in0=m.A1[:, 0:128], scalar=m.anm[:, 2:3],
                                                  in1=m.ax[:, :], op0=ALU.mult, op1=ALU.add))
                    moments(m.hand_a[:, 0, :], m.ast[:, :], m.amv[:, :], s["a_var"])
                if slot == 7:
                    dve.wait_ge(s["a_rstd"], 2)
                    normalize(m.ah[:, :], m.hand_a[:, 0, :], m.amv, m.arstd).then_inc(s["a_h2"], 1)
                for i in range(16):
                    if slot == 13 + (4 * i) // 3:
                        dve.wait_ge(s["a_sims"], i // 4 + 1)
                        top16(m.top[:, i, :], m.topi[:, i, :], m.sims[:, i, :])
                if slot == 34:
                    pairs(m.cs[:, :, :], m.top[:, 0:HEADS, :], m.top[:, HEADS:16, :], 0, 0)
                if slot == 35:
                    step(dve.tensor_copy(m.idxf[:, :, :, :].rearrange("p a h k -> p (a h) k"), m.topi[:, :, :]))
                    step(dve.scalar_tensor_tensor(out=m.idxf[:, 1, :, :], in0=m.idxf[:, 1, :, :], scalar=float(KEYS),
                                                  in1=m.hoff[:, :, :], op0=ALU.mult, op1=ALU.add))
                    pairs(m.ci[:, :, :], m.idxf[:, 0, :, :], m.idxf[:, 1, :, :], 0, 0)
                if 36 <= slot < 36 + 3 * HEADS:
                    h, part = divmod(slot - 36, 3)
                    if part == 0:
                        top16(m.fin[:, h, :], m.pos[:, :], m.cs[:, h, :])
                        step(dve.tensor_copy(m.posf[:, :], m.pos[:, :]))
                    else:
                        for k in range(8 * part - 8, 8 * part):
                            step(dve.scalar_tensor_tensor(
                                out=m.junk[:, k % JUNK, :], in0=m.iota[:, :], scalar=m.posf[:, k:k + 1],
                                in1=m.ci[:, h, :], op0=ALU.is_equal, op1=ALU.mult,
                                accum_out=m.chosen[:, h, k:k + 1]))
                if slot == 60:
                    step(dve.tensor_copy(m.idx_a[:, :], m.chosen[:, :, :].rearrange("p h k -> p (h k)")))
                    step(dve.tensor_copy(m.wsum[:, :], m.fin[:, :, 0]))
                    dve.tensor_tensor(m.fin[:, :, :], m.fin[:, :, :], over(m.wsum[:, :], 128, HEADS, TOPK, 2),
                                      ALU.subtract).then_inc(s["a_wdiff"], 1)
                if slot == 61:
                    dve.wait_ge(s["a_wexp"], 1)
                    step(dve.tensor_reduce(m.wsum[:, :], m.fin[:, :, :], AX.X, ALU.add))
                    step(dve.reciprocal(m.wsum[:, :], m.wsum[:, :]))
                    step(dve.tensor_tensor(m.w_a[:, :].rearrange("p (h k) -> p h k", h=HEADS), m.fin[:, :, :],
                                           over(m.wsum[:, :], 128, HEADS, TOPK, 2), ALU.mult))

            def stage_g(slot):
                n, second = divmod(slot - G_LAG, 2)
                if not 0 <= n < HEADS * GROUPS or n // GROUPS % 2:
                    return
                h, r = divmod(n, GROUPS)
                if not second:
                    dve.wait_ge(s["gathered"][n % RING], gathered_by(n))
                for k in (2 * second, 2 * second + 1):
                    i = h * TOPK + r * GROUP + k
                    row, weight, acc = m.ring[:, n % RING, k, :], m.w_g[:, i:i + 1], m.kv_g[:, h, :]
                    if r == 0 and k == 0:
                        if h == 0 and do_c:
                            dve.wait_ge(s["hand_kv"], 1)
                        step(dve.tensor_scalar(acc, row, weight, None, ALU.mult))
                    else:
                        step(dve.scalar_tensor_tensor(out=acc, in0=row, scalar=weight, in1=acc,
                                                      op0=ALU.mult, op1=ALU.add))
                if second:
                    dve.sem_inc(s["g_vec_used"], 1)

            def stage_c(k):
                if k == 0:
                    dve.wait_ge(s["c_adj_in"], 16)
                    step(dve.tensor_scalar(m.cbias[:, :], m.cadj[:, :], 0.0, 1.0, ALU.is_gt, ALU.subtract))
                    step(dve.tensor_scalar(m.cbias[:, :], m.cbias[:, :], -MASKED, None, ALU.mult))
                if k in (5, 6):
                    half = k - 5
                    dve.wait_ge(s["c_s_ps"], half + 1)
                    step(dve.scalar_tensor_tensor(out=m.catt[:, 4 * half:4 * half + 4, :],
                                                  in0=heads4((m.C0, m.C1)[half]), scalar=float(D) ** -0.5,
                                                  in1=over(m.causal[:, :], 128, 4, 128, 1),
                                                  op0=ALU.mult, op1=ALU.add))
                if k == 6:
                    dve.tensor_reduce(m.cnm[:, :], m.catt[:, :, :], AX.X, ALU.max, negate=True).then_inc(s["c_max"], 1)
                if k == 7:
                    dve.wait_ge(s["c_p"], 1)
                    step(dve.reciprocal(m.crs[:, :], m.csum[:, :]))
                    dve.tensor_tensor(m.catt[:, :, :], m.catt[:, :, :], over(m.crs[:, :], 128, HEADS, 128, 2),
                                      ALU.mult).then_inc(s["c_pn"], 1)
                if k == 12:
                    dve.wait_ge(s["c_wo"], 1)
                    step(dve.tensor_tensor(m.cx2[:, :], m.C0[:, 0:D], m.hand_c[:, 0, :], ALU.add))
                    moments(m.cx2[:, :], m.cst[:, :], m.cmv[:, :], s["c_var"])
                if k == 13:
                    dve.wait_ge(s["c_rstd"], 1)
                    step(normalize(m.cy[:, :], m.cx2[:, :], m.cmv, m.crstd))
                    moments(m.cy[:, :], m.cst[:, :], m.cmv[:, :], s["c_var"])
                if k == 14:
                    dve.wait_ge(s["c_rstd"], 2)
                    normalize(m.cn[:, :], m.cy[:, :], m.cmv, m.crstd).then_inc(s["c_n"], 1)
                    dve.wait_ge(s["c_n"], 1)
                    step(dve.tensor_tensor(m.cqkv[:, :], m.cn[:, :], p["g1_row"], ALU.mult))
                    dve.tensor_tensor(m.cqkv[:, :], m.cqkv[:, :], p["be1_row"], ALU.add).then_inc(s["c_qkv"], 1)
                if k == 15:
                    dve.wait_ge(s["c_nT"], 1)
                    dve.tensor_tensor(m.cqm[:, :, :], over(m.cnT[:, :], 128, GH, 128, 1),
                                      over(m.headmask[:, :], 128, GH, 128, 2), ALU.mult).then_inc(s["c_qm"], 1)
                if k in (16, 17):
                    half = k - 16
                    dve.wait_ge(s["c_g_ps"], half + 1)
                    step(dve.scalar_tensor_tensor(out=m.catt[:, 4 * half:4 * half + 4, :],
                                                  in0=heads4((m.C0, m.C1)[half]), scalar=float(GD) ** -0.5,
                                                  in1=over(m.cbias[:, :], 128, 4, 128, 1),
                                                  op0=ALU.mult, op1=ALU.add))
                if k == 17:
                    dve.tensor_reduce(m.cnm[:, :], m.catt[:, :, :], AX.X, ALU.max, negate=True).then_inc(s["c_gmax"], 1)
                if k == 18:
                    dve.wait_ge(s["c_gp"], 1)
                    step(dve.reciprocal(m.crs[:, :], m.csum[:, :]))
                if k == 21:
                    dve.wait_ge(s["c_go"], 1)
                    step(dve.tensor_tensor(m.cxp[:, :].rearrange("p (h c) -> p h c", h=GH),
                                           m.C0[:, 0:128].rearrange("p (h c) -> p h c", h=GH),
                                           over(m.crs[:, :], 128, GH, GD, 2), ALU.mult))
                    step(dve.tensor_tensor(m.cxp[:, :], m.cxp[:, :], m.cy[:, :], ALU.add))
                    moments(m.cxp[:, :], m.cst[:, :], m.cmv[:, :], s["c_var"])
                if k == 22:
                    dve.wait_ge(s["c_rstd"], 3)
                    normalize(m.cn[:, :], m.cxp[:, :], m.cmv, m.crstd).then_inc(s["c_n2"], 1)
                    step(dve.tensor_tensor(m.cres[:, :], m.cxp[:, :], m.cx2[:, :], ALU.add))
                    step(dve.tensor_tensor(m.cres[:, :], m.cres[:, :], p["b2_row"], ALU.add))
                if k == 25:
                    dve.wait_ge(s["c_mlp"], 1)
                    step(dve.tensor_tensor(m.x3_c[:, :], m.C1[:, 0:D], m.cres[:, :], ALU.add))

            def sigmoid_of(e):
                step(dve.tensor_scalar(e, e, 1.0, None, ALU.add))
                step(dve.reciprocal(e, e))

            def stage_d(k):
                if k == 0:
                    moments(m.x3_d[:, :], m.dst6[:, :], m.dmv[:, :], s["d_var"])
                if k == 1:
                    dve.wait_ge(s["d_rstd"], 1)
                    normalize(m.du[:, :], m.x3_d[:, :], m.dmv, m.drstd).then_inc(s["d_u"], 1)
                    step(dve.tensor_tensor(m.dres[:, :], m.x3_d[:, :], p["outb_row"], ALU.add))
                if k == 3:
                    dve.wait_ge(s["d_l_ps"], 1)
                    step(dve.tensor_tensor(m.dz[:, :, :].rearrange("p h g -> p (h g)"), m.D1[:, :], m.lbias[:, :],
                                           ALU.add))
                    step(dve.tensor_reduce(m.dnm[:, :], m.dz[:, :, :], AX.X, ALU.max, negate=True))
                    dve.tensor_tensor(m.dz[:, :, :], m.dz[:, :, :], over(m.dnm[:, :], 128, SH, SL, 2),
                                      ALU.add).then_inc(s["d_z"], 1)
                if k == 4:
                    dve.wait_ge(s["d_fx_ps"], 1)
                    dve.tensor_tensor(m.dfx[:, :, 0:SP_], m.D0[:, :].rearrange("p (h c) -> p h c", h=SH),
                                      p["bfx_row"].rearrange("p (h c) -> p h c", h=SH), ALU.add)
                    dve.wait_ge(s["d_e"], 1)
                    step(dve.tensor_reduce(m.dnm[:, :], m.dsw[:, :, :], AX.X, ALU.add))
                    step(dve.reciprocal(m.dnm[:, :], m.dnm[:, :]))
                    dve.tensor_tensor(m.dsw[:, :, :], m.dsw[:, :, :], over(m.dnm[:, :], 128, SH, SL, 2),
                                      ALU.mult).then_inc(s["d_sw"], 1)
                if k == 5:
                    dve.wait_ge(s["d_st_ps"], 1)
                    sums = [bank[0:64, 0:4 * (SP_ + 1)].rearrange("p (h c) -> p h c", h=4) for bank in (m.D0, m.D1)]
                    for half in range(2):
                        step(dve.tensor_scalar(m.dden[:, 4 * half:4 * half + 4], sums[half][:, :, SP_], EPS, None,
                                               ALU.add))
                    step(dve.reciprocal(m.dden[:, :], m.dden[:, :]))
                    for half in range(2):
                        last = dve.tensor_tensor(m.dstn[:, 4 * half:4 * half + 4, :], sums[half][:, :, 0:SP_],
                                                 over(m.dden[:, 4 * half:4 * half + 4], 64, 4, SP_, 2), ALU.mult)
                    last.then_inc(s["d_stn"], 1)
                if k == 7:
                    dve.wait_ge(s["d_dt_ps"], 1)
                    step(dve.tensor_tensor(m.ddt[:, :], m.D0[0:64, 0:2 * SH], p["dtb_row"][0:64], ALU.add))
                    step(dve.tensor_scalar(m.ddtm[:, :], m.ddt[:, :], 0.0, None, ALU.max))
                    dve.scalar_tensor_tensor(out=m.ddta[:, :], in0=m.ddt[:, :], scalar=-1.0, in1=m.ddt[:, :],
                                             op0=ALU.mult, op1=ALU.min).then_inc(s["d_dta"], 1)
                    dve.wait_ge(s["d_z_ps"], 1)
                    dve.tensor_scalar(m.dzc[:, :], m.D2[0:64, :], -CLAMP, None, ALU.max).then_inc(s["d_zc"], 1)
                if k == 8:
                    dve.wait_ge(s["d_ln"], 1)
                    step(dve.tensor_tensor(m.ddt[:, :], m.ddta[:, :], m.ddtm[:, :], ALU.add))
                    dve.tensor_tensor(m.ddA[:, :], m.ddt[:, :], m.ea[:, :], ALU.mult).then_inc(s["d_dtA"], 1)
                    dve.wait_ge(s["d_tap"], 1)
                    for tap in (1, 0):
                        for q in range(6):
                            rows = 128 if q < 4 else 64
                            last = dve.scalar_tensor_tensor(
                                out=m.dxc[0:rows, q, :], in0=m.dxp[0:rows, q, tap:tap + SL],
                                scalar=p["convw"][0:rows, 3 * q + tap:3 * q + tap + 1],
                                in1=m.dxc[0:rows, q, :], op0=ALU.mult, op1=ALU.add)
                        step(last)
                    dve.tensor_scalar(m.dex[:, :, :], m.dxc[:, :, :], -CLAMP, None, ALU.max).then_inc(s["d_xcl"], 1)
                    dve.wait_ge(s["d_ez"], 1)
                    sigmoid_of(m.dzc[:, :])
                    step(dve.tensor_tensor(m.dsilz[:, :], m.D2[0:64, :], m.dzc[:, :], ALU.mult))
                if k == 9:
                    dve.wait_ge(s["d_dA"], 1)
                    for way, ident in enumerate((m.identf, m.identb)):
                        last = dve.tensor_tensor(m.ded[:, way, :, :], over(ident[:, :], 64, SH, SL, 1),
                                                 over(m.ddA[:, SH * way:SH * (way + 1)], 64, SH, SL, 2), ALU.mult)
                    last.then_inc(s["d_ed"], 1)
                    dve.wait_ge(s["d_ex"], 1)
                    sigmoid_of(m.dex[:, :, :])
                    dve.tensor_tensor(m.dxc[:, :, :], m.dxc[:, :, :], m.dex[:, :, :], ALU.mult).then_inc(s["d_xc"], 1)
                if k == 10:
                    dve.wait_ge(s["d_DA_ps"], 1)
                    flat = m.dL[:, :, :, :].rearrange("p w h t -> p w (h t)")
                    starts = m.identrep[:, :, :].rearrange("p h t -> p (h t)")
                    dve.tensor_tensor_scan(flat[:, 0, :], m.D1[0:64, :], starts, 0.0, ALU.mult, ALU.add)
                    step(dve.tensor_tensor_scan(flat[:, 1, ::-1], m.D2[0:64, ::-1], starts[:, ::-1], 0.0,
                                                ALU.mult, ALU.add))
                    dve.wait_ge(s["d_Gs"], 1)
                    for way in range(2):
                        last = dve.tensor_tensor(m.dL[:, way, :, :], m.dL[:, way, :, :],
                                                 over(m.dG[:, :], 64, SH, SL, 1), ALU.mult)
                    step(last)
                    for way, out in enumerate((m.dMf[:, :, 1:SL + 1], m.dMb[:, :, 0:SL])):
                        last = dve.tensor_tensor(out, m.dL[:, way, :, :],
                                                 over(m.ddt[:, SH * way:SH * (way + 1)], 64, SH, SL, 2), ALU.mult)
                    last.then_inc(s["d_M"], 1)
                if k == 11:
                    dve.wait_ge(s["d_fd_ps"], 1)
                    step(dve.tensor_tensor(m.dfd[:, :], m.D0[0:64, 0:SH], p["dp_row"][0:64], ALU.add))
                if k == 12:
                    dve.wait_ge(s["d_xn"], 1)
                    step(dve.tensor_tensor(m.dyg[:, :, :], m.dxn[:, :, :], over(m.dfd[:, :], 64, SH, SP_, 2), ALU.mult))
                    dve.wait_ge(s["d_y_ps"], 1)
                    step(dve.tensor_tensor(m.dyg[:, :, :], m.D2[0:64, :].rearrange("p (h c) -> p h c", h=SH),
                                           m.dyg[:, :, :], ALU.add))
                    dve.tensor_tensor(m.dyg[:, :, :], m.dyg[:, :, :],
                                      m.dsilz[:, :].rearrange("p (h c) -> p h c", h=SH), ALU.mult).then_inc(s["d_yg"], 1)
                if k == 13:
                    dve.wait_ge(s["d_rr"], 1)
                    dve.tensor_scalar(m.dyg[:, :, :], m.dyg[:, :, :], m.dss[:, 0:1], None, ALU.mult)\
                        .then_inc(s["d_ygn"], 1)
                if k == 17:
                    dve.wait_ge(s["d_f_ps"], 1)
                    dve.tensor_tensor(m.dout[:, :], m.D0[:, 0:D], m.dres[:, :], ALU.add).then_inc(s["d_out"], 1)

            if do_g:
                dve.tensor_copy(m.idx_g[:, :], m.idx_a[:, :]).then_inc(s["hand_idx"], 1)
                dve.tensor_copy(m.w_g[:, :], m.w_a[:, :]).then_inc(s["hand_w"], 1)
            if do_d:
                step(dve.tensor_copy(m.x3_d[:, :], m.x3_c[:, :]))
            if do_c:
                dve.tensor_copy(m.hand_c[:, :, :], m.hand_g[:, :, :]).then_inc(s["hand_h2T"], 1)
                dve.wait_ge(s["hand_h2T"], 1)
            if do_g:
                step(dve.tensor_copy(m.hand_g[:, :, :], m.hand_a[:, :, :]))
            for slot in range(SLOTS):
                if do_a:
                    stage_a(slot)
                if do_c and slot in c_at:
                    stage_c(c_at[slot])
                if do_d and slot in d_at:
                    stage_d(d_at[slot])
                if do_g:
                    stage_g(slot)


def two_layers(nc, x, adj, table, params, factors, out, graphs=B):
    dram = {"x": x, "adj": adj, "table": table, "out": out}
    with ExitStack() as ctx:
        m = lay_out_memory(nc, ctx)
        s = {name: ctx.enter_context(nc.semaphore(name)) for name in SIGNALS}
        s["gathered"] = [ctx.enter_context(nc.semaphore(f"gathered{i}")) for i in range(RING)]
        first, last = s["load_done"].num, s["d_stored"].num
        assert last - first + 1 == len(SIGNALS)

        def again():
            nc.vector.sem_clear(range(first, last + 1))
            nc.all_engine_barrier(sem_only=True)

        set_up(nc, m, s, params, factors)
        again()
        turn(nc, m, s, dram, a=0)
        again()
        turn(nc, m, s, dram, a=1, g=0)
        again()
        turn(nc, m, s, dram, a=2, g=1, c=0)
        again()
        if graphs > 3:
            with nc.Fori(3, graphs) as a:
                turn(nc, m, s, dram, a=a, g=a - 1, c=a - 2, d=a - 3)
                again()
        turn(nc, m, s, dram, g=graphs - 1, c=graphs - 2, d=graphs - 3)
        again()
        turn(nc, m, s, dram, c=graphs - 1, d=graphs - 2)
        again()
        turn(nc, m, s, dram, d=graphs - 1)


def lay_out_inputs(i):
    import numpy as np

    f = {k: np.asarray(v) for k, v in i.items()}

    def chunks(w, n):
        return w.reshape(n, -1, w.shape[-1]).transpose(1, 0, 2).reshape(w.shape[0] // n, -1)

    def rows(v, n=128):
        return np.broadcast_to(v.reshape(1, -1), (n, v.size))

    def fill(table, parts, made):
        cols = []
        for name, width in table:
            v = made[name]
            assert v.shape[1] == width, (name, v.shape, width)
            if v.shape[0] < parts:
                v = np.concatenate([v, np.zeros((parts - v.shape[0], width), v.dtype)])
            cols.append(v)
        return np.ascontiguousarray(np.concatenate(cols, 1))

    def conv(w):
        zero = np.zeros((64, w.shape[1]), w.dtype)
        w = np.concatenate([w[:DI + NS], zero, w[DI + NS:], zero])
        return chunks(w, 6)

    params = fill(PARAMS, 128, {
        "a_cols": np.stack([f[f"L0_gnn_a{k}"] for k in range(4)], 1),
        "wq": f["L0_ffn_Wq"],
        "wo": chunks(f["L0_ffn_Wo"], HEADS),
        "gb_cols": np.stack([f[f"L1_gnn_{k}"] for k in ("gamma1", "beta1", "gamma2", "beta2")], 1),
        "b1_cols": f["L1_gnn_b1"].reshape(FF, 128).T,
        "g1_row": rows(f["L1_gnn_gamma1"]), "be1_row": rows(f["L1_gnn_beta1"]),
        "b2_row": rows(f["L1_gnn_b2"]), "outb_row": rows(f["L1_ffn_out_b"]),
        "w1": f["L1_gnn_W1"], "w2": chunks(f["L1_gnn_W2"], FF),
        "wfx": f["L1_ffn_W_fx"].T, "bfx_row": rows(f["L1_ffn_b_fx"]),
        "bslice_row": rows(f["L1_ffn_b_slice"]), "temp_row": rows(f["L1_ffn_temperature"]),
        "inw": chunks(f["L1_ffn_hy_in_w"].T, KC),
        "convw": conv(f["L1_ffn_hy_conv_w"]), "convb": conv(f["L1_ffn_hy_conv_b"][:, None]),
        "dtb_row": rows(np.concatenate([f["L1_ffn_hy_dt_bias"]] * 2)),
        "alog_row": rows(np.concatenate([f["L1_ffn_hy_A_log"]] * 2)),
        "fcd": chunks(f["L1_ffn_hy_fcD_w"].T, KC), "dp_row": rows(f["L1_ffn_hy_D"]),
        "normw": chunks(f["L1_ffn_hy_norm_w"][:, None], KC), "hyout": chunks(f["L1_ffn_hy_out_w"].T, KC),
        "outw": chunks(f["L1_ffn_out_w"].T, KC),
    })
    factors = fill(FACTORS, 64, {
        "wqpk_t": f["L0_ffn_Wq_pk"].T.reshape(16, DK, D).transpose(1, 0, 2).reshape(DK, -1),
        "keys_t": f["L0_ffn_pk_keys"].transpose(3, 0, 2, 1).reshape(DK, -1),
        "wx": chunks(f["L1_ffn_W_x"], SH), "bx": f["L1_ffn_b_x"].reshape(SH, SP_).T,
        "wslice_t": f["L1_ffn_W_slice"].T,
    })
    table = np.concatenate([f["L0_ffn_keys_table"], f["L0_ffn_values_table"]], 1)
    return {"x": f["x"], "adj": f["adj"], "table": table, "params": params, "factors": factors}


def kernel(**inputs):
    import concourse.bacc as _bacc
    from concourse.bass_utils import run_bass_kernel_spmd as _run

    nc = _bacc.Bacc("TRN2", target_bir_lowering=False, num_devices=1)
    arrays = lay_out_inputs(inputs)
    args = {n: nc.dram_tensor(n, a.shape, mybir.dt.from_np(a.dtype), kind="ExternalInput").ap()
            for n, a in arrays.items()}
    out = nc.dram_tensor("out", (B, T, D), F32, kind="ExternalOutput").ap()
    two_layers(nc, out=out, **args)
    return _run(nc, [arrays], core_ids=[0]).results[0]["out"]
```

```python
from contextlib import ExitStack

import concourse.bass as bass
from concourse import mybir

F32 = mybir.dt.float32
I32 = mybir.dt.int32
U32 = mybir.dt.uint32
ALU = mybir.AluOpType
ACT = mybir.ActivationFunctionType
AX = mybir.AxisListType

B, T, D = 64, 128, 128
HEADS, DK = 8, 64
KEYS, TOPK = 128, 16
ROW = 2 * D
NK_HEAD = KEYS * KEYS
GH, GD = 8, 16
FF = 4 * D // 128
SH, SL, SP_ = 8, 64, 64
DI = SH * SP_
NS = 64
KC = DI // 128
PROJ = 2 * DI + 2 * NS + 2 * SH
XBC, DT = DI, 2 * DI + 2 * NS
EPS = 1e-5
LOWEST = -3.4028235e38
MASKED = -3.0e38
NEG_INF = -9000000000000000.0
SLOPE = 0.2
TEMP_MIN = 1e-6
LOG_MAX = 80.0
EXP_LN = "natural_log_exp_and_others"

RECTS = [(0, 1, 16), (1, 1, 8), (2, 2, 5), (4, 4, 3), (8, 8, 1)]
CAND = sum(r * c for _, r, c in RECTS)

GROUP = 4
GROUPS = TOPK // GROUP
RING = 8
G_LAG = 3
SLOTS = 2 * HEADS * GROUPS
EARLY = 6
CARRIED = 2
IN_TURN = HEADS * GROUPS - CARRIED
DIAGS, DIAG_AHEAD = 4, 6
JUNK = 4
FOLD_KEYS, FOLD = 6, 14
FINAL, FINAL_SLOTS = 36, 5
VECTOR_HEADS = (0, 2)

PARAMS = [
    ("a_cols", 4), ("wq", HEADS * D), ("wo", HEADS * D), ("gb_cols", 4), ("b1_cols", FF),
    ("g1_row", D), ("be1_row", D), ("b2_row", D), ("outb_row", D), ("w1", FF * 128), ("w2", FF * D),
    ("wfx", DI), ("bfx_row", DI), ("bslice_row", SL), ("temp_row", SH), ("inw", KC * PROJ),
    ("convw", 6 * 3), ("convb", 6), ("dtb_row", 2 * SH), ("alog_row", 2 * SH), ("fcd", KC * SH),
    ("dp_row", SH), ("normw", KC), ("hyout", KC * DI), ("outw", KC * D),
]
FACTORS = [("wqpk_t", 16 * D), ("keys_t", 16 * KEYS), ("wx", SH * D), ("bx", SH), ("wslice_t", SL)]


class Tiles:
    pass


def places(table):
    at, found = 0, {}
    for name, width in table:
        found[name] = (at, at + width)
        at += width
    return found, at


TENSOR_HEADS = tuple(h for h in range(HEADS) if h not in VECTOR_HEADS)


def groups_before(h, r):
    heads = VECTOR_HEADS if h in VECTOR_HEADS else TENSOR_HEADS
    return heads.index(h) * GROUPS + r


PARAM_AT, PARAM_COLS = places(PARAMS)
FACTOR_AT, FACTOR_COLS = places(FACTORS)
A_COLS = PARAM_AT["a_cols"][1]
KEY_COLS = FACTOR_AT["keys_t"][1]

SIGNALS = """
cols_in keys_in load_done const_done fold_row fold_mm fold_keys fold_out
vector_steps scalar_steps
early_idx hand_idx hand_w hand_h2T hand_kv
a_x_in a_adj_in a_var a_rstd a_h a_hT_ps a_hTa a_scores a_alpha a_p a_pT_ps a_pT a_o a_h2
a_h2T_ps a_h2T a_sim_ps a_sims a_wdiff a_wexp
g_vec_used g_pe_used g_carried g_diag g_head
c_adj_in c_q_ps c_q c_k_ps c_k c_s_ps c_max c_p c_rs c_pn c_pT_ps c_pT c_o_ps c_o c_wo c_var c_rstd
c_n c_nT_ps c_nT c_qkv c_qm c_g_ps c_gmax c_gp c_gpT_ps c_gpT c_go c_n2 c_n2T_ps c_y2T
c_hid_ps c_gelu c_mlp
d_var d_rstd d_u d_uT_ps d_uT d_l_ps d_z d_e d_fx_ps d_sw d_st_ps d_stn d_swT_ps d_swT
d_stT_ps d_stT d_z_ps d_x_ps d_dt_ps d_xp d_dta d_silz d_tap d_ln d_dtA d_conv d_dA
d_xc d_DA_ps d_G_ps d_Gs d_M d_xn_ps d_fd_ps d_xn d_y_ps d_yg d_rr d_ygn d_ygT_ps d_ygT d_ot_ps
d_obd d_R_ps d_R d_f_ps d_out d_stored
""".split()


class Chain:

    def __init__(self, engine, semaphore):
        self.engine, self.semaphore, self.n = engine, semaphore, 0

    def ready(self, behind=0):
        if self.n > behind:
            self.engine.wait_ge(self.semaphore, self.n - behind)

    def did(self, instruction):
        self.n += 1
        instruction.then_inc(self.semaphore, 1)


def over(ap, parts, rows, cols, dim):
    return ap.unsqueeze(dim).broadcast_to([parts, rows, cols])


def lay_out_memory(nc, ctx):
    def sb(name, shape, dtype=F32):
        return ctx.enter_context(nc.sbuf_tensor(name, shape, dtype))

    m = Tiles()
    m.params = sb("params_sb", [128, PARAM_COLS])
    m.p = {k: m.params[:, a:b] for k, (a, b) in PARAM_AT.items()}
    m.ring = sb("ring", [128, RING, GROUP, ROW])
    m.factors = m.ring[0:64].rearrange("p a b c -> p (a b c)")[:, 0:FACTOR_COLS]
    m.f = {k: m.factors[:, a:b] for k, (a, b) in FACTOR_AT.items()}
    m.wsim = sb("wsim", [128, 16 * KEYS])
    m.wslice = sb("wslice", [128, SH * SL])
    m.lbias = sb("lbias", [128, SH * SL])
    m.ea = sb("ea", [64, 2 * SH])
    m.invt = sb("invt", [128, SH])
    m.ident = sb("ident", [128, 128])
    m.causal = sb("causal", [128, 128])
    m.headmask = sb("headmask", [128, GH])
    m.identf = sb("identf", [64, 64])
    m.identb = sb("identb", [64, 64])
    m.identrep = sb("identrep", [64, SH, SL])
    m.iota = sb("iota", [128, CAND])
    m.hoff = sb("hoff", [128, HEADS, TOPK])
    m.eps = sb("eps", [128, 1])
    m.one = sb("one", [128, 1])
    m.hand_a = sb("hand_a", [128, 2, 128])
    m.hand_g = sb("hand_g", [128, 2, 128])
    m.hand_c = sb("hand_c", [128, 2, 128])
    m.idx_a = sb("idx_a", [128, HEADS * TOPK], U32)
    m.idx_g = sb("idx_g", [128, HEADS * TOPK], U32)
    m.idx_l = sb("idx_l", [128, CARRIED * GROUP], U32)
    m.w_a = sb("w_a", [128, HEADS * TOPK])
    m.w_g = sb("w_g", [128, HEADS * TOPK])
    m.kv_g = sb("kv_g", [128, HEADS, ROW])
    m.kv_c = sb("kv_c", [128, HEADS, ROW])
    m.x3_c = sb("x3_c", [128, 128])
    m.x3_d = sb("x3_d", [128, 128])
    m.ax = sb("ax", [128, 128])
    m.aadj = sb("aadj", [128, 128], I32)
    m.ast = sb("ast", [128, 6])
    m.amv = sb("amv", [128, 2])
    m.arstd = sb("arstd", [128, 2])
    m.ah = sb("ah", [128, 128])
    m.ahT = sb("ahT", [128, 128])
    m.ahTa = sb("ahTa", [128, 4, 128])
    m.amask = sb("amask", [128, 4, 128], I32)
    m.alpha = sb("alpha", [128, 128])
    m.anm = sb("anm", [128, 4])
    m.ap = sb("ap", [128, 128])
    m.apT = sb("apT", [128, 128])
    m.sims = sb("sims", [128, 16, KEYS])
    m.top = sb("top", [128, 16, TOPK])
    m.topi = sb("topi", [128, 16, TOPK], U32)
    m.idxf = sb("idxf", [128, 2, HEADS, TOPK])
    m.cs = sb("cs", [128, HEADS, CAND])
    m.ci = sb("ci", [128, HEADS, CAND])
    m.fin = sb("fin", [128, HEADS, TOPK])
    m.pos = sb("pos", [128, 2, TOPK], U32)
    m.posf = sb("posf", [128, 2, TOPK])
    m.junk = sb("junk", [128, JUNK, CAND])
    m.chosen = sb("chosen", [128, HEADS, TOPK])
    m.wsum = sb("wsum", [128, HEADS])
    m.diag = sb("diag", [128, DIAGS, GROUP, 128])
    m.cadj = sb("cadj", [128, 128], I32)
    m.cbias = sb("cbias", [128, 128])
    m.cq = sb("cq", [128, HEADS, 128])
    m.ck = sb("ck", [128, HEADS, 128])
    m.catt = sb("catt", [128, HEADS, 128])
    m.cpT = sb("cpT", [128, HEADS, 128])
    m.coT = m.cq
    m.cnm = sb("cnm", [128, HEADS])
    m.csum = sb("csum", [128, HEADS])
    m.crs = sb("crs", [128, HEADS])
    m.cx2 = sb("cx2", [128, 128])
    m.cst = sb("cst", [128, 6])
    m.cmv = sb("cmv", [128, 2])
    m.crstd = sb("crstd", [128, 2])
    m.cy = sb("cy", [128, 128])
    m.cn = sb("cn", [128, 128])
    m.cnT = sb("cnT", [128, 128])
    m.cqkv = sb("cqkv", [128, 128])
    m.cqm = m.ck
    m.cxp = sb("cxp", [128, 128])
    m.cres = sb("cres", [128, 128])
    m.cy2T = sb("cy2T", [128, 128])
    m.cgT = sb("cgT", [128, FF, 128])
    m.dst6 = sb("dst6", [128, 6])
    m.dmv = sb("dmv", [128, 2])
    m.drstd = sb("drstd", [128, 2])
    m.du = sb("du", [128, 128])
    m.duT = sb("duT", [128, 128])
    m.dres = sb("dres", [128, 128])
    m.dz = sb("dz", [128, SH, SL])
    m.dnm = sb("dnm", [128, SH])
    m.dsw = sb("dsw", [128, SH, SL])
    m.dfx = sb("dfx", [128, SH, SP_ + 1])
    m.dden = sb("dden", [64, SH])
    m.dstn = sb("dstn", [64, SH, SP_])
    m.dswT = sb("dswT", [128, KC, 128])
    m.dstT = sb("dstT", [128, KC, 64])
    m.dxp = sb("dxp", [128, 6, SL + 2])
    m.dxc = sb("dxc", [128, 6, SL])
    m.ddt = sb("ddt", [64, 2 * SH])
    m.ddtm = sb("ddtm", [64, 2 * SH])
    m.ddta = sb("ddta", [64, 2 * SH])
    m.ddA = sb("ddA", [64, 2 * SH])
    m.dsilz = m.dstn[:, :, :].rearrange("p h c -> p (h c)")
    m.dL = sb("dL", [64, 2, SH, SL])
    m.dG = sb("dG", [64, SL])
    m.dMf = sb("dMf", [64, SH, SL + 1])
    m.dMb = sb("dMb", [64, SH, SL + 1])
    m.dxn = m.dz[0:64]
    m.dfd = sb("dfd", [64, SH])
    m.dyg = sb("dyg", [64, SH, SP_])
    m.dsq = m.dL[:, 0, :, :].rearrange("p h t -> p (h t)")
    m.dss = sb("dss", [64, 2])
    m.dygT = sb("dygT", [128, KC, 64])
    m.dobd = sb("dobd", [128, KC, 128])
    m.dR = sb("dR", [128, KC, 128])
    m.dout = m.dres
    for_name = lambda name: ctx.enter_context(nc.psum_tensor(name, [128, 512], F32))
    m.A0, m.A1, m.G0 = for_name("A0"), for_name("A1"), for_name("G0")
    m.C0, m.C1 = for_name("C0"), for_name("C1")
    m.D0, m.D1, m.D2 = for_name("D0"), for_name("D1"), for_name("D2")
    return m


def heads4(bank, n=128):
    return bank[:, 0:4 * n].rearrange("p (h n) -> p h n", h=4)


def set_up(nc, m, s, dram):
    with nc.Block(no_gpsimd_drain=True) as block:

        @block.sync
        def _(sp):
            sp.dma_start(m.ax[:, :], dram["x"][0]).then_inc(s["a_x_in"], 16)
            sp.dma_start(m.p["a_cols"], dram["params"][:, 0:A_COLS]).then_inc(s["cols_in"], 16)
            sp.dma_start(m.aadj[:, :], dram["adj"][0]).then_inc(s["a_adj_in"], 16)
            sp.dma_start(m.factors[:, 0:KEY_COLS], dram["factors"][:, 0:KEY_COLS]).then_inc(s["keys_in"], 16)

        @block.gpsimd
        def _(pool):
            def const(instruction, n=[0]):
                n[0] += 1
                instruction.then_inc(s["const_done"], 1)
                pool.wait_ge(s["const_done"], n[0])

            const(pool.memset(m.ident[:, :], 0.0))
            const(pool.affine_select(out=m.ident[:, :], in_=m.ident[:, :], compare_op=ALU.not_equal, fill=1.0,
                                     base=0, pattern=[[-1, 128]], channel_multiplier=1))
            const(pool.memset(m.causal[:, :], 0.0))
            const(pool.affine_select(out=m.causal[:, :], in_=m.causal[:, :], compare_op=ALU.is_ge, fill=MASKED,
                                     base=0, pattern=[[-1, 128]], channel_multiplier=1))
            const(pool.memset(m.headmask[:, :], 1.0))
            const(pool.affine_select(out=m.headmask[:, :], in_=m.headmask[:, :], compare_op=ALU.is_ge, fill=0.0,
                                     base=0, pattern=[[-GD, GH]], channel_multiplier=1))
            const(pool.affine_select(out=m.headmask[:, :], in_=m.headmask[:, :], compare_op=ALU.is_ge, fill=0.0,
                                     base=GD - 1, pattern=[[GD, GH]], channel_multiplier=-1))
            const(pool.iota(m.iota[:, :], pattern=[[1, CAND]], base=0, channel_multiplier=0,
                            allow_small_or_imprecise_dtypes=True))
            const(pool.iota(m.hoff[:, :, :], pattern=[[NK_HEAD, HEADS], [0, TOPK]], base=0, channel_multiplier=0,
                            allow_small_or_imprecise_dtypes=True))
            for tile in (m.dMf, m.dMb, m.dxp, m.dobd):
                const(pool.memset(tile[:, :, :], 0.0))
            const(pool.memset(m.dfx[:, :, :], 1.0))
            const(pool.memset(m.dxc[:, :, :], 0.0))

        @block.vector
        def _(dve):
            dve.memset(m.eps[:, :], EPS)
            dve.memset(m.one[:, :], 1.0)


def turn(nc, m, s, dram, a=None, g=None, c=None, d=None, fold=False, finish=False):
    do_a, do_g, do_c, do_d = a is not None, g is not None, c is not None, d is not None
    p = m.p

    def gathered_by(graph, n):
        per_turn = HEADS * GROUPS // RING
        return (graph * per_turn + n // RING + 1) * (16 * GROUP)

    c_at = {(9 * k) // 4: k for k in range(26)}
    d_at = {3 * k + 1: k for k in range(18)}

    with nc.Block(no_gpsimd_drain=True) as block:

        @block.sync
        def _(sp):
            if do_a and not fold:
                sp.dma_start(m.ax[:, :], dram["x"][a]).then_inc(s["a_x_in"], 16)
                sp.dma_start(m.aadj[:, :], dram["adj"][a]).then_inc(s["a_adj_in"], 16)
            if fold:
                sp.dma_start(m.params[:, A_COLS:], dram["params"][:, A_COLS:]).then_inc(s["load_done"], 16)
                sp.dma_start(m.factors[:, KEY_COLS:], dram["factors"][:, KEY_COLS:]).then_inc(s["load_done"], 16)
            if do_c:
                sp.dma_start(m.cadj[:, :], dram["adj"][c]).then_inc(s["c_adj_in"], 16)
            if do_d:
                sp.wait_ge(s["d_out"], 1)
                sp.dma_start(dram["out"][d], m.dout[:, :]).then_inc(s["d_stored"], 16)
                sp.wait_ge(s["d_stored"], 16)

        @block.gpsimd
        def _(pool):
            def gather(n, columns):
                for k in range(GROUP):
                    pool.indirect_dma_start(
                        out=m.ring[:, n % RING, k, :], out_offset=None, in_=dram["table"],
                        in_offset=bass.IndirectOffsetOnAxis(ap=columns[:, k:k + 1], axis=0),
                    ).then_inc(s["gathered"][n % RING], 16)

            if fold:
                pool.wait_ge(s["fold_mm"], 2)
                pool.wait_ge(s["early_idx"], 1)
                for n in range(EARLY):
                    gather(n, m.idx_a[:, n * GROUP:(n + 1) * GROUP])
            if not do_g:
                return
            pool.wait_ge(s["hand_idx"], 1)
            for n in range(EARLY if finish else 0, HEADS * GROUPS):
                h, r = divmod(n, GROUPS)
                if n >= RING:
                    before = h - RING // GROUPS
                    used = s["g_vec_used"] if before in VECTOR_HEADS else s["g_pe_used"]
                    pool.wait_ge(used, groups_before(before, r) + 1)
                elif n >= RING - CARRIED and do_c:
                    pool.wait_ge(s["g_carried"], n - (RING - CARRIED) + 1)
                if n == IN_TURN:
                    pool.wait_ge(s["hand_idx"], 2)
                late = n - IN_TURN
                gather(n, m.idx_l[:, late * GROUP:(late + 1) * GROUP] if late >= 0
                       else m.idx_g[:, n * GROUP:(n + 1) * GROUP])

        @block.tensor
        def _(pe):
            def transpose(out, in_, n):
                return pe.transpose(out, in_, m.ident[0:n, 0:n])

            def stage_a(slot):
                if slot == 2:
                    pe.wait_ge(s["a_h"], 1)
                    transpose(m.A0[:, 0:128], m.ah[:, :], 128).then_inc(s["a_hT_ps"], 1)
                if slot == 3:
                    pe.wait_ge(s["a_hTa"], 1)
                    pe.matmul(m.A1[:, :], m.ahT[:, :], m.ahTa[:, :, :], start=True, stop=True).then_inc(s["a_scores"], 1)
                if slot == 5:
                    pe.wait_ge(s["a_p"], 1)
                    transpose(m.A0[:, 0:128], m.ap[:, :], 128).then_inc(s["a_pT_ps"], 1)
                if slot == 6:
                    pe.wait_ge(s["a_pT"], 1)
                    pe.matmul(m.A1[:, 0:128], m.apT[:, :], m.ah[:, :], start=True, stop=True).then_inc(s["a_o"], 1)
                if slot == 8:
                    pe.wait_ge(s["a_h2"], 1)
                    transpose(m.A0[:, 0:128], m.ah[:, :], 128).then_inc(s["a_h2T_ps"], 1)
                if 9 <= slot < 13:
                    k = slot - 9
                    if fold and k == 0:
                        pe.wait_ge(s["fold_keys"], 1)
                    pe.wait_ge(s["a_h2T"], 1)
                    if k >= 2:
                        pe.wait_ge(s["a_sims"], k - 1)
                    pe.matmul((m.A1, m.A0)[k % 2][:, :], m.hand_a[:, 1, :], m.wsim[:, 512 * k:512 * (k + 1)],
                              start=True, stop=True).then_inc(s["a_sim_ps"], 1)

            def sum_group(h, r, n):
                for k in range(GROUP):
                    last = pe.matmul(m.G0[:, 0:ROW], m.diag[:, groups_before(h, r) % DIAGS, k, :],
                                     m.ring[:, n % RING, k, :],
                                     start=(r == 0 and k == 0), stop=(r == GROUPS - 1 and k == GROUP - 1))
                return last

            def stage_g(slot):
                n, second = divmod(slot - G_LAG, 2)
                if second or not 0 <= n < IN_TURN or n // GROUPS in VECTOR_HEADS:
                    return
                h, r = divmod(n, GROUPS)
                i = TENSOR_HEADS.index(h)
                pe.wait_ge(s["gathered"][n % RING], gathered_by(g, n))
                pe.wait_ge(s["g_diag"], groups_before(h, r) + 1)
                if r == 0 and i > 0:
                    pe.wait_ge(s["g_head"], i)
                elif r == 0 and do_c:
                    pe.wait_ge(s["hand_kv"], 1)
                sum_group(h, r, n).then_inc(s["g_pe_used"], 1)

            def stage_c(k):
                if k in (1, 2):
                    half = k - 1
                    pe.wait_ge(s["hand_h2T"], 1)
                    bank = heads4((m.C0, m.C1)[half])
                    for j in range(4):
                        h = 4 * half + j
                        last = pe.matmul(bank[:, j, :], p["wq"][:, D * h:D * (h + 1)], m.hand_c[:, 1, :],
                                         start=True, stop=True)
                    last.then_inc(s["c_q_ps"], 1)
                if k in (3, 4):
                    half = k - 3
                    pe.wait_ge(s["hand_kv"], 1)
                    pe.wait_ge(s["c_q"], half + 1)
                    bank = heads4((m.C0, m.C1)[half])
                    for j in range(4):
                        last = transpose(bank[:, j, :], m.kv_c[:, 4 * half + j, 0:D], 128)
                    last.then_inc(s["c_k_ps"], 1)
                if k in (5, 6):
                    half = k - 5
                    pe.wait_ge(s["c_k"], half + 1)
                    bank = heads4((m.C0, m.C1)[half])
                    for j in range(4):
                        h = 4 * half + j
                        last = pe.matmul(bank[:, j, :], m.cq[:, h, :], m.ck[:, h, :], start=True, stop=True)
                    last.then_inc(s["c_s_ps"], 1)
                if k in (8, 9):
                    half = k - 8
                    pe.wait_ge(s["c_pn"], 1)
                    bank = heads4((m.C0, m.C1)[half])
                    for j in range(4):
                        last = transpose(bank[:, j, :], m.catt[:, 4 * half + j, :], 128)
                    last.then_inc(s["c_pT_ps"], 1)
                if k in (10, 11):
                    half = k - 10
                    pe.wait_ge(s["c_pT"], half + 1)
                    bank = heads4((m.C0, m.C1)[half])
                    for j in range(4):
                        h = 4 * half + j
                        last = pe.matmul(bank[:, j, :], m.kv_c[:, h, D:ROW], m.cpT[:, h, :], start=True, stop=True)
                    last.then_inc(s["c_o_ps"], 1)
                if k == 12:
                    pe.wait_ge(s["c_o"], 2)
                    for h in range(HEADS):
                        last = pe.matmul(m.C0[:, 0:D], m.coT[:, h, :], p["wo"][:, D * h:D * (h + 1)],
                                         start=(h == 0), stop=(h == HEADS - 1))
                    last.then_inc(s["c_wo"], 1)
                if k == 15:
                    pe.wait_ge(s["c_n"], 1)
                    transpose(m.C1[:, 0:128], m.cn[:, :], 128).then_inc(s["c_nT_ps"], 1)
                if k in (16, 17):
                    half = k - 16
                    pe.wait_ge(s["c_qm"], 1)
                    pe.matmul((m.C0, m.C1)[half][:, :], m.cnT[:, :], m.cqm[:, 4 * half:4 * half + 4, :],
                              start=True, stop=True).then_inc(s["c_g_ps"], 1)
                if k in (19, 20):
                    half = k - 19
                    pe.wait_ge(s["c_gp"], 1)
                    bank = heads4((m.C0, m.C1)[half])
                    for j in range(4):
                        last = transpose(bank[:, j, :], m.catt[:, 4 * half + j, :], 128)
                    last.then_inc(s["c_gpT_ps"], 1)
                if k == 21:
                    pe.wait_ge(s["c_gpT"], 2)
                    pe.wait_ge(s["c_qkv"], 1)
                    for h in range(GH):
                        cols = slice(GD * h, GD * (h + 1))
                        last = pe.matmul(m.C0[:, cols], m.cpT[:, h, :], m.cqkv[:, cols], start=True, stop=True)
                    last.then_inc(s["c_go"], 1)
                if k == 23:
                    pe.wait_ge(s["c_n2"], 1)
                    transpose(m.C1[:, 0:128], m.cn[:, :], 128).then_inc(s["c_n2T_ps"], 1)
                if k == 24:
                    pe.wait_ge(s["c_y2T"], 1)
                    for f in range(FF):
                        last = pe.matmul(m.C0[:, 128 * f:128 * (f + 1)], p["w1"][:, 128 * f:128 * (f + 1)],
                                         m.cy2T[:, :], start=True, stop=True)
                    last.then_inc(s["c_hid_ps"], 1)
                if k == 25:
                    pe.wait_ge(s["c_gelu"], 1)
                    for f in range(FF):
                        last = pe.matmul(m.C1[:, 0:D], m.cgT[:, f, :], p["w2"][:, D * f:D * (f + 1)],
                                         start=(f == 0), stop=(f == FF - 1))
                    last.then_inc(s["c_mlp"], 1)

            def stage_d(k):
                inw = p["inw"].rearrange("p (k n) -> p k n", k=KC)
                if k == 2:
                    pe.wait_ge(s["d_u"], 1)
                    transpose(m.D0[:, 0:128], m.du[:, :], 128).then_inc(s["d_uT_ps"], 1)
                if k == 3:
                    pe.wait_ge(s["d_uT"], 1)
                    pe.matmul(m.D1[:, :], m.duT[:, :], m.wslice[:, :], start=True, stop=True).then_inc(s["d_l_ps"], 1)
                if k == 4:
                    pe.matmul(m.D0[:, :], m.duT[:, :], p["wfx"], start=True, stop=True).then_inc(s["d_fx_ps"], 1)
                if k == 5:
                    pe.wait_ge(s["d_sw"], 1)
                    for h in range(SH):
                        cols = slice((SP_ + 1) * (h % 4), (SP_ + 1) * (h % 4 + 1))
                        last = pe.matmul((m.D0, m.D1)[h // 4][0:64, cols], m.dsw[:, h, :], m.dfx[:, h, :],
                                         start=True, stop=True)
                    last.then_inc(s["d_st_ps"], 1)
                if k == 6:
                    for j in range(KC):
                        last = transpose(m.D2[:, 128 * j:128 * (j + 1)],
                                         m.dsw[:, 2 * j:2 * j + 2, :].rearrange("p a b -> p (a b)"), 128)
                    last.then_inc(s["d_swT_ps"], 1)
                    pe.wait_ge(s["d_stn"], 1)
                    for j in range(KC):
                        last = transpose(m.D0[:, 64 * j:64 * (j + 1)],
                                         m.dstn[:, 2 * j:2 * j + 2, :].rearrange("p a b -> p (a b)"), 64)
                    last.then_inc(s["d_stT_ps"], 1)
                if k == 7:
                    pe.wait_ge(s["d_stT"], 1)
                    for j in range(KC):
                        last = pe.matmul(m.D0[0:64, 0:2 * SH], m.dstT[:, j, :], inw[:, j, DT:PROJ],
                                         start=(j == 0), stop=(j == KC - 1))
                    last.then_inc(s["d_dt_ps"], 1)
                    for q in range(6):
                        first = XBC + 128 * min(q, 4) + 64 * (q == 5)
                        rows = 128 if q < 4 else 64
                        for j in range(KC):
                            last = pe.matmul(m.D1[0:rows, 64 * q:64 * (q + 1)], inw[:, j, first:first + rows],
                                             m.dstT[:, j, :], start=(j == 0), stop=(j == KC - 1))
                    last.then_inc(s["d_x_ps"], 1)
                    pe.wait_ge(s["d_swT"], 1)
                    for j in range(KC):
                        last = pe.matmul(m.D2[0:64, :], m.dstT[:, j, :], inw[:, j, 0:DI],
                                         start=(j == 0), stop=(j == KC - 1))
                    last.then_inc(s["d_z_ps"], 1)
                if k == 10:
                    pe.wait_ge(s["d_silz"], 1)
                    pe.wait_ge(s["d_dA"], 1)
                    for bank, way, ident in ((m.D1, 0, m.identf), (m.D2, 1, m.identb)):
                        for h in range(SH):
                            dA = m.ddA[:, SH * way + h:SH * way + h + 1].broadcast_to([64, SL])
                            last = pe.matmul(bank[0:64, SL * h:SL * (h + 1)], dA, ident[:, :], start=True, stop=True)
                    last.then_inc(s["d_DA_ps"], 1)
                    pe.wait_ge(s["d_xc"], 1)
                    pe.matmul(m.D0[0:64, 0:SL], m.dxc[0:64, 4, :], m.dxc[0:64, 5, :], start=True, stop=True)\
                        .then_inc(s["d_G_ps"], 1)
                if k == 11:
                    pe.wait_ge(s["d_Gs"], 1)
                    fcd = p["fcd"].rearrange("p (k n) -> p k n", k=KC)
                    for j in range(KC):
                        last = pe.matmul(m.D0[0:64, 0:SH], m.dxc[:, j, :], fcd[:, j, :],
                                         start=(j == 0), stop=(j == KC - 1))
                    last.then_inc(s["d_fd_ps"], 1)
                    pe.wait_ge(s["d_M"], 1)
                    for j in range(KC):
                        last = transpose(m.D1[0:64, 128 * j:128 * (j + 1)], m.dxc[:, j, :], 128)
                    last.then_inc(s["d_xn_ps"], 1)
                if k == 12:
                    pe.wait_ge(s["d_xn"], 1)
                    for h in range(SH):
                        cols = slice(SP_ * h, SP_ * (h + 1))
                        pe.matmul(m.D2[0:64, cols], m.dMf[:, h, 0:SL], m.dxn[:, h, :], start=True, stop=False)
                        last = pe.matmul(m.D2[0:64, cols], m.dMb[:, h, 1:SL + 1], m.dxn[:, h, :],
                                         start=False, stop=True)
                    last.then_inc(s["d_y_ps"], 1)
                if k == 14:
                    pe.wait_ge(s["d_ygn"], 1)
                    for j in range(KC):
                        last = transpose(m.D0[:, 64 * j:64 * (j + 1)],
                                         m.dyg[:, 2 * j:2 * j + 2, :].rearrange("p a b -> p (a b)"), 64)
                    last.then_inc(s["d_ygT_ps"], 1)
                if k == 15:
                    pe.wait_ge(s["d_ygT"], 1)
                    hyout = p["hyout"].rearrange("p (k n) -> p k n", k=KC)
                    for q in range(KC):
                        for j in range(KC):
                            last = pe.matmul(m.D1[:, 64 * q:64 * (q + 1)], hyout[:, j, 128 * q:128 * (q + 1)],
                                             m.dygT[:, j, :], start=(j == 0), stop=(j == KC - 1))
                    last.then_inc(s["d_ot_ps"], 1)
                if k == 16:
                    pe.wait_ge(s["d_obd"], 1)
                    for q in range(KC):
                        last = pe.matmul(m.D2[:, 128 * q:128 * (q + 1)], m.dobd[:, q, :],
                                         p["outw"][:, D * q:D * (q + 1)], start=True, stop=True)
                    last.then_inc(s["d_R_ps"], 1)
                if k == 17:
                    pe.wait_ge(s["d_R"], 1)
                    for q in range(KC):
                        last = pe.matmul(m.D0[:, 0:D], m.dswT[:, q, :], m.dR[:, q, :],
                                         start=(q == 0), stop=(q == KC - 1))
                    last.then_inc(s["d_f_ps"], 1)

            if do_c:
                for n in range(IN_TURN, HEADS * GROUPS):
                    pe.wait_ge(s["gathered"][n % RING], gathered_by(c, n))
                    sum_group(HEADS - 1, n % GROUPS, n).then_inc(s["g_carried"], 1)
            def fold_keys():
                pe.wait_ge(s["keys_in"], 16)
                for i in range(16):
                    bank = (m.C0, m.C1, m.D0, m.D1)[i // 4]
                    last = pe.matmul(bank[:, 128 * (i % 4):128 * (i % 4 + 1)],
                                     m.f["wqpk_t"][:, 128 * i:128 * (i + 1)],
                                     m.f["keys_t"][:, 128 * i:128 * (i + 1)], start=True, stop=True)
                last.then_inc(s["fold_mm"], 1)

            def fold_slices():
                pe.wait_ge(s["load_done"], 32)
                pe.wait_ge(s["fold_keys"], 1)
                pe.wait_ge(s["fold_out"], 1)
                for h in range(SH):
                    cols = slice(SL * h, SL * (h + 1))
                    pe.matmul(m.D0[:, cols], m.f["wx"][:, D * h:D * (h + 1)], m.f["wslice_t"], start=True, stop=True)
                    last = pe.matmul(m.D1[:, cols], m.catt[0:64, h, :], m.f["wslice_t"], start=True, stop=True)
                last.then_inc(s["fold_mm"], 1)

            for slot in range(SLOTS):
                if do_a:
                    stage_a(slot)
                if fold and slot == FOLD_KEYS:
                    fold_keys()
                if fold and slot == FOLD:
                    fold_slices()
                if do_c and slot in c_at:
                    stage_c(c_at[slot])
                if do_d and slot in d_at:
                    stage_d(d_at[slot])
                if do_g:
                    stage_g(slot)

        @block.scalar
        def _(act):
            steps = Chain(act, s["scalar_steps"])

            def copy(out, in_):
                return act.activation(out, in_, ACT.Copy)

            def rstd(out, mv, ready):
                steps.did(act.activation(out[:, 0:1], mv[:, 1:2], ACT.Ln, bias=m.eps[:, :]))
                steps.ready()
                act.activation(out[:, 1:2], out[:, 0:1], ACT.Exp, scale=-0.5).then_inc(ready, 1)

            def stage_a(slot):
                if slot == 1:
                    act.wait_ge(s["a_var"], 1)
                    rstd(m.arstd, m.amv, s["a_rstd"])
                if slot == 2:
                    act.wait_ge(s["a_hT_ps"], 1)
                    copy(m.ahT[:, :], m.A0[:, 0:128])
                    if fold:
                        act.wait_ge(s["cols_in"], 16)
                    for k in range(4):
                        last = act.activation(m.ahTa[:, k, :], m.A0[:, 0:128], ACT.Copy, scale=p["a_cols"][:, k:k + 1])
                    last.then_inc(s["a_hTa"], 1)
                if slot == 4:
                    act.wait_ge(s["a_alpha"], 1)
                    act.activation(m.ap[:, :], m.alpha[:, :], ACT.Exp, bias=m.anm[:, 0:1],
                                   accum_out=m.anm[:, 1:2]).then_inc(s["a_p"], 1)
                if slot == 5:
                    act.wait_ge(s["a_pT_ps"], 1)
                    copy(m.apT[:, :], m.A0[:, 0:128]).then_inc(s["a_pT"], 1)
                if slot == 7:
                    act.wait_ge(s["a_var"], 2)
                    rstd(m.arstd, m.amv, s["a_rstd"])
                if slot == 8:
                    act.wait_ge(s["a_h2T_ps"], 1)
                    copy(m.hand_a[:, 1, :], m.A0[:, 0:128]).then_inc(s["a_h2T"], 1)
                if 9 <= slot < 13:
                    k = slot - 9
                    act.wait_ge(s["a_sim_ps"], k + 1)
                    copy(m.sims[:, 4 * k:4 * k + 4, :], heads4((m.A1, m.A0)[k % 2])).then_inc(s["a_sims"], 1)
                if slot == FINAL + HEADS // 2 * FINAL_SLOTS + 1:
                    act.wait_ge(s["a_wdiff"], 1)
                    act.activation(m.fin[:, :, :], m.fin[:, :, :], ACT.Exp).then_inc(s["a_wexp"], 1)

            def diagonals(slot):
                n, second = divmod(slot - G_LAG + DIAG_AHEAD, 2)
                if second or not 0 <= n < HEADS * GROUPS or n // GROUPS in VECTOR_HEADS:
                    return
                h, r = divmod(n, GROUPS)
                before = groups_before(h, r)
                if before == 0:
                    act.wait_ge(s["hand_w"], 1)
                if before >= DIAGS:
                    act.wait_ge(s["g_pe_used"], before - DIAGS + 1)
                for k in range(GROUP):
                    at = h * TOPK + r * GROUP + k
                    last = act.activation(m.diag[:, before % DIAGS, k, :], m.ident[:, :], ACT.Copy,
                                          scale=m.w_g[:, at:at + 1])
                last.then_inc(s["g_diag"], 1)

            def stage_g(slot):
                n, second = divmod(slot - G_LAG, 2)
                h, r = divmod(n, GROUPS)
                if not second or r != GROUPS - 1 or h not in TENSOR_HEADS:
                    return
                act.wait_ge(s["g_pe_used"], groups_before(h, r) + 1)
                if h == TENSOR_HEADS[0] and do_c:
                    act.wait_ge(s["hand_kv"], 1)
                copy(m.kv_g[:, h, :], m.G0[:, 0:ROW]).then_inc(s["g_head"], 1)

            def exps(ready):
                for h in range(HEADS):
                    last = act.activation(m.catt[:, h, :], m.catt[:, h, :], ACT.Exp, bias=m.cnm[:, h:h + 1],
                                          accum_out=m.csum[:, h:h + 1])
                last.then_inc(ready, 1)

            def normalize_rows():
                act.wait_ge(s["c_rs"], 1)
                for h in range(HEADS):
                    last = act.activation(m.catt[:, h, :], m.catt[:, h, :], ACT.Copy, scale=m.crs[:, h:h + 1])
                last.then_inc(s["c_pn"], 1)

            def stage_c(k):
                for first, at, ready, out in ((1, s["c_q_ps"], s["c_q"], m.cq), (3, s["c_k_ps"], s["c_k"], m.ck),
                                              (8, s["c_pT_ps"], s["c_pT"], m.cpT), (10, s["c_o_ps"], s["c_o"], m.coT),
                                              (19, s["c_gpT_ps"], s["c_gpT"], m.cpT)):
                    if k in (first, first + 1):
                        half = k - first
                        act.wait_ge(at, half + 1)
                        copy(out[:, 4 * half:4 * half + 4, :], heads4((m.C0, m.C1)[half])).then_inc(ready, 1)
                if k == 7:
                    act.wait_ge(s["c_max"], 1)
                    exps(s["c_p"])
                if k in (13, 14):
                    act.wait_ge(s["c_var"], k - 12)
                    rstd(m.crstd, m.cmv, s["c_rstd"])
                if k == 15:
                    act.wait_ge(s["c_nT_ps"], 1)
                    act.activation(m.cnT[:, :], m.C1[:, 0:128], ACT.Identity, bias=p["gb_cols"][:, 1:2],
                                   scale=p["gb_cols"][:, 0:1]).then_inc(s["c_nT"], 1)
                    act.wait_ge(s["c_nT"], 1)
                    for h in range(GH):
                        last = act.activation(m.cqm[:, h, :], m.cnT[:, :], ACT.Copy, scale=m.headmask[:, h:h + 1])
                    last.then_inc(s["c_qm"], 1)
                if k == 18:
                    act.wait_ge(s["c_gmax"], 1)
                    exps(s["c_gp"])
                if k == 22:
                    act.wait_ge(s["c_var"], 3)
                    rstd(m.crstd, m.cmv, s["c_rstd"])
                if k == 23:
                    act.wait_ge(s["c_n2T_ps"], 1)
                    act.activation(m.cy2T[:, :], m.C1[:, 0:128], ACT.Identity, bias=p["gb_cols"][:, 3:4],
                                   scale=p["gb_cols"][:, 2:3]).then_inc(s["c_y2T"], 1)
                if k == 24:
                    act.wait_ge(s["c_hid_ps"], 1)
                    for f in range(FF):
                        last = act.activation(m.cgT[:, f, :], m.C0[:, 128 * f:128 * (f + 1)], ACT.Gelu,
                                              bias=p["b1_cols"][:, f:f + 1])
                    last.then_inc(s["c_gelu"], 1)
                    act.preload_act_table_set(EXP_LN)

            def stage_d(k):
                if k == 1:
                    act.wait_ge(s["d_var"], 1)
                    rstd(m.drstd, m.dmv, s["d_rstd"])
                if k == 2:
                    act.wait_ge(s["d_uT_ps"], 1)
                    copy(m.duT[:, :], m.D0[:, 0:128]).then_inc(s["d_uT"], 1)
                if k == 4:
                    act.wait_ge(s["d_z"], 1)
                    act.activation(m.dsw[:, :, :], m.dz[:, :, :], ACT.Exp).then_inc(s["d_e"], 1)
                if k == 6:
                    act.wait_ge(s["d_swT_ps"], 1)
                    copy(m.dswT[:, :, :], heads4(m.D2)).then_inc(s["d_swT"], 1)
                    act.wait_ge(s["d_stT_ps"], 1)
                    copy(m.dstT[:, :, :], heads4(m.D0, 64)).then_inc(s["d_stT"], 1)
                if k == 7:
                    act.wait_ge(s["d_x_ps"], 1)
                    copy(m.dxp[:, 0:4, 2:SL + 2], heads4(m.D1, 64))
                    copy(m.dxp[0:64, 4:6, 2:SL + 2], m.D1[0:64, 256:384].rearrange("p (a b) -> p a b", a=2))\
                        .then_inc(s["d_xp"], 1)
                if k == 8:
                    act.wait_ge(s["d_dta"], 1)
                    steps.did(act.activation(m.ddta[:, :], m.ddta[:, :], ACT.Exp))
                    steps.ready()
                    act.activation(m.ddta[:, :], m.ddta[:, :], ACT.Ln, bias=m.one[0:64, :]).then_inc(s["d_ln"], 1)
                    act.wait_ge(s["d_xp"], 1)
                    for q in range(6):
                        rows = 128 if q < 4 else 64
                        last = act.activation(m.dxc[0:rows, q, :], m.dxp[0:rows, q, 2:SL + 2], ACT.Identity,
                                              bias=p["convb"][0:rows, q:q + 1],
                                              scale=p["convw"][0:rows, 3 * q + 2:3 * q + 3])
                    last.then_inc(s["d_tap"], 1)
                if k == 9:
                    act.wait_ge(s["d_dtA"], 1)
                    act.activation(m.ddA[:, :], m.ddA[:, :], ACT.Exp, scale=-1.0).then_inc(s["d_dA"], 1)
                    act.wait_ge(s["d_z_ps"], 1)
                    act.activation(m.dsilz, m.D2[0:64, :], ACT.Silu).then_inc(s["d_silz"], 1)
                    act.wait_ge(s["d_conv"], 1)
                    act.activation(m.dxc[:, :, :], m.dxc[:, :, :], ACT.Silu).then_inc(s["d_xc"], 1)
                    act.preload_act_table_set(EXP_LN)
                if k == 10:
                    act.wait_ge(s["d_G_ps"], 1)
                    copy(m.dG[:, :], m.D0[0:64, 0:SL]).then_inc(s["d_Gs"], 1)
                if k == 11:
                    act.wait_ge(s["d_xn_ps"], 1)
                    copy(m.dxn[:, :, :], m.D1[0:64, :].rearrange("p (h c) -> p h c", h=SH)).then_inc(s["d_xn"], 1)
                if k == 13:
                    act.wait_ge(s["d_yg"], 1)
                    steps.did(act.activation(m.dsq, m.dyg[:, :, :].rearrange("p h c -> p (h c)"), ACT.Square,
                                             accum_out=m.dss[:, 0:1]))
                    steps.ready()
                    steps.did(act.activation(m.dss[:, 1:2], m.dss[:, 0:1], ACT.Ln, bias=m.eps[0:64, :],
                                             scale=1.0 / DI))
                    steps.ready()
                    act.activation(m.dss[:, 0:1], m.dss[:, 1:2], ACT.Exp, scale=-0.5).then_inc(s["d_rr"], 1)
                if k == 14:
                    act.wait_ge(s["d_ygT_ps"], 1)
                    copy(m.dygT[:, :, :], heads4(m.D0, 64)).then_inc(s["d_ygT"], 1)
                if k == 15:
                    act.wait_ge(s["d_ot_ps"], 1)
                    copy(m.dobd[0:64, :, 0:64], m.D1[0:64, 0:256].rearrange("p (q g) -> p q g", q=KC))
                    copy(m.dobd[64:128, :, 64:128], m.D1[64:128, 0:256].rearrange("p (q g) -> p q g", q=KC))\
                        .then_inc(s["d_obd"], 1)
                if k == 16:
                    act.wait_ge(s["d_R_ps"], 1)
                    copy(m.dR[:, :, :], heads4(m.D2)).then_inc(s["d_R"], 1)

            def fold_keys():
                act.wait_ge(s["fold_mm"], 1)
                for c, bank in enumerate((m.C0, m.C1, m.D0, m.D1)):
                    last = copy(m.wsim[:, 512 * c:512 * (c + 1)], bank[:, :])
                last.then_inc(s["fold_keys"], 1)

            def fold_slices():
                act.wait_ge(s["load_done"], 32)
                copy(m.catt[0:64, :, :], over(m.f["bx"], 64, SH, 128, 2)).then_inc(s["fold_out"], 1)
                for k in range(KC):
                    cols = p["hyout"][:, DI * k:DI * (k + 1)]
                    act.activation(cols, cols, ACT.Copy, scale=p["normw"][:, k:k + 1])\
                        .then_inc(s["scalar_steps"], 1)
                steps.n += KC

            def finish_weights():
                act.wait_ge(s["fold_row"], 1)
                steps.did(act.activation(m.ea[:, :], m.ea[:, :], ACT.Exp))

            act.preload_act_table_set(EXP_LN)
            if do_c:
                copy(m.kv_c[:, 0:HEADS - 1, :], m.kv_g[:, 0:HEADS - 1, :])
                act.wait_ge(s["g_carried"], CARRIED)
                copy(m.kv_c[:, HEADS - 1, :], m.G0[:, 0:ROW]).then_inc(s["hand_kv"], 1)
            for slot in range(SLOTS):
                if do_g:
                    diagonals(slot)
                if do_a:
                    stage_a(slot)
                if fold and slot == FOLD_KEYS:
                    fold_keys()
                if fold and slot == FOLD:
                    fold_slices()
                if finish and slot == FOLD:
                    finish_weights()
                if do_c and slot - 1 in c_at and c_at[slot - 1] == 7:
                    normalize_rows()
                if do_c and slot in c_at:
                    stage_c(c_at[slot])
                if do_d and slot in d_at:
                    stage_d(d_at[slot])
                if do_g:
                    stage_g(slot)

        @block.vector
        def _(dve):
            chain = Chain(dve, s["vector_steps"])

            def step(instruction):
                chain.did(instruction)
                chain.ready()

            def moments(x, stats, mv, ready):
                step(dve.bn_stats(stats, x))
                dve.bn_aggr(mv, stats).then_inc(ready, 1)

            def normalize(out, x, mv, rstd):
                return dve.tensor_scalar(out, x, mv[:, 0:1], rstd[:, 1:2], ALU.subtract, ALU.mult)

            def top16(rows):
                every = len(rows) - 1
                for first in (0, 8):
                    for scores, values, at in rows:
                        chain.ready(every)
                        chain.did(dve.max(values[:, first:first + 8], scores))
                    for scores, values, at in rows:
                        chain.ready(every)
                        chain.did(dve.max_index(at[:, first:first + 8], values[:, first:first + 8], scores))
                    if first == 0:
                        for scores, values, at in rows:
                            chain.ready(every)
                            chain.did(dve.match_replace(scores, values[:, 0:8], scores, LOWEST))

            def pairs(out, first, second):
                at = 0
                for i0, rows, cols in RECTS:
                    o = out[:, :, at:at + rows * cols].rearrange("p h (i j) -> p h i j", i=rows)
                    x = first[:, :, i0:i0 + rows].unsqueeze(3).broadcast_to([128, HEADS, rows, cols])
                    y = second[:, :, 0:cols].unsqueeze(2).broadcast_to([128, HEADS, rows, cols])
                    if rows == 1:
                        o, x, y = o[:, :, 0, :], x[:, :, 0, :], y[:, :, 0, :]
                    if cols == 1:
                        o, x, y = o[:, :, :, 0], x[:, :, :, 0], y[:, :, :, 0]
                    chain.did(dve.tensor_tensor(o, x, y, ALU.add))
                    at += rows * cols

            def stage_a(slot):
                if slot == 0:
                    dve.wait_ge(s["a_x_in"], 16)
                    moments(m.ax[:, :], m.ast[:, :], m.amv[:, :], s["a_var"])
                if slot == 1:
                    dve.wait_ge(s["a_rstd"], 1)
                    normalize(m.ah[:, :], m.ax[:, :], m.amv, m.arstd).then_inc(s["a_h"], 1)
                    dve.wait_ge(s["a_adj_in"], 16)
                    for k in range(4):
                        dve.tensor_scalar(m.amask[:, k, :], m.aadj[:, :], float(k + 1), None, ALU.is_equal)
                    step(dve.memset(m.alpha[:, :], NEG_INF / SLOPE))
                if slot == 3:
                    dve.wait_ge(s["a_scores"], 1)
                    for k in range(4):
                        step(dve.copy_predicated(m.alpha[:, :], m.amask[:, k, :], m.A1[:, 128 * k:128 * (k + 1)]))
                    step(dve.scalar_tensor_tensor(out=m.alpha[:, :], in0=m.alpha[:, :], scalar=SLOPE,
                                                  in1=m.alpha[:, :], op0=ALU.mult, op1=ALU.max))
                    dve.tensor_reduce(m.anm[:, 0:1], m.alpha[:, :], AX.X, ALU.max, negate=True).then_inc(s["a_alpha"], 1)
                if slot == 4:
                    dve.wait_ge(s["a_p"], 1)
                    step(dve.reciprocal(m.anm[:, 2:3], m.anm[:, 1:2]))
                if slot == 6:
                    dve.wait_ge(s["a_o"], 1)
                    step(dve.scalar_tensor_tensor(out=m.hand_a[:, 0, :], in0=m.A1[:, 0:128], scalar=m.anm[:, 2:3],
                                                  in1=m.ax[:, :], op0=ALU.mult, op1=ALU.add))
                    moments(m.hand_a[:, 0, :], m.ast[:, :], m.amv[:, :], s["a_var"])
                if slot == 7:
                    dve.wait_ge(s["a_rstd"], 2)
                    normalize(m.ah[:, :], m.hand_a[:, 0, :], m.amv, m.arstd).then_inc(s["a_h2"], 1)
                for i in range(0, 16, 2):
                    if slot == 13 + (4 * i) // 3:
                        dve.wait_ge(s["a_sims"], i // 4 + 1)
                        top16([(m.sims[:, j, :], m.top[:, j, :], m.topi[:, j, :]) for j in (i, i + 1)])
                if slot == 33:
                    chain.ready()
                    pairs(m.cs[:, :, :], m.top[:, 0:HEADS, :], m.top[:, HEADS:16, :])
                if slot == 34:
                    step(dve.tensor_copy(m.idxf[:, :, :, :].rearrange("p a h k -> p (a h) k"), m.topi[:, :, :]))
                    step(dve.scalar_tensor_tensor(out=m.idxf[:, 1, :, :], in0=m.idxf[:, 1, :, :], scalar=float(KEYS),
                                                  in1=m.hoff[:, :, :], op0=ALU.mult, op1=ALU.add))
                    pairs(m.ci[:, :, :], m.idxf[:, 0, :, :], m.idxf[:, 1, :, :])
                if slot == FINAL - 1:
                    chain.ready()
                    chain.did(dve.tensor_copy(m.chosen[:, :, 0], m.ci[:, :, 0]))
                if FINAL <= slot < FINAL + HEADS // 2 * FINAL_SLOTS:
                    pair, part = divmod(slot - FINAL, FINAL_SLOTS)
                    two = (2 * pair, 2 * pair + 1)
                    if fold and (pair, part) == (1, 0):
                        chain.ready()
                        dve.tensor_copy(m.idx_a[:, 0:2 * TOPK], m.chosen[:, 0:2, :].rearrange("p h k -> p (h k)"))\
                            .then_inc(s["early_idx"], 1)
                    if part == 0:
                        chain.ready()
                        top16([(m.cs[:, h, :], m.fin[:, h, :], m.pos[:, h % 2, :]) for h in two])
                        chain.ready()
                        step(dve.tensor_copy(m.posf[:, :, :], m.pos[:, :, :]))
                    looked_up = [(h, k) for k in range(1, TOPK) for h in two]
                    for h, k in looked_up[part - 1::FINAL_SLOTS - 1] if part else ():
                        chain.ready(JUNK - 1)
                        chain.did(dve.scalar_tensor_tensor(
                            out=m.junk[:, chain.n % JUNK, :], in0=m.iota[:, :], scalar=m.posf[:, h % 2, k:k + 1],
                            in1=m.ci[:, h, :], op0=ALU.is_equal, op1=ALU.mult,
                            accum_out=m.chosen[:, h, k:k + 1]))
                if slot == FINAL + HEADS // 2 * FINAL_SLOTS:
                    chain.ready()
                    rest = 2 * TOPK if fold else 0
                    step(dve.tensor_copy(m.idx_a[:, rest:], m.chosen[:, :, :].rearrange("p h k -> p (h k)")[:, rest:]))
                    step(dve.tensor_copy(m.wsum[:, :], m.fin[:, :, 0]))
                    dve.tensor_tensor(m.fin[:, :, :], m.fin[:, :, :], over(m.wsum[:, :], 128, HEADS, TOPK, 2),
                                      ALU.subtract).then_inc(s["a_wdiff"], 1)
                if slot == FINAL + HEADS // 2 * FINAL_SLOTS + 1:
                    dve.wait_ge(s["a_wexp"], 1)
                    step(dve.tensor_reduce(m.wsum[:, :], m.fin[:, :, :], AX.X, ALU.add))
                    step(dve.reciprocal(m.wsum[:, :], m.wsum[:, :]))
                    step(dve.tensor_tensor(m.w_a[:, :].rearrange("p (h k) -> p h k", h=HEADS), m.fin[:, :, :],
                                           over(m.wsum[:, :], 128, HEADS, TOPK, 2), ALU.mult))

            def stage_g(slot):
                n, second = divmod(slot - G_LAG, 2)
                if not 0 <= n < HEADS * GROUPS or n // GROUPS not in VECTOR_HEADS:
                    return
                h, r = divmod(n, GROUPS)
                if not second:
                    dve.wait_ge(s["gathered"][n % RING], gathered_by(g, n))
                for k in (2 * second, 2 * second + 1):
                    i = h * TOPK + r * GROUP + k
                    row, weight, acc = m.ring[:, n % RING, k, :], m.w_g[:, i:i + 1], m.kv_g[:, h, :]
                    if r == 0 and k == 0:
                        if h == 0 and do_c:
                            dve.wait_ge(s["hand_kv"], 1)
                        step(dve.tensor_scalar(acc, row, weight, None, ALU.mult))
                    else:
                        step(dve.scalar_tensor_tensor(out=acc, in0=row, scalar=weight, in1=acc,
                                                      op0=ALU.mult, op1=ALU.add))
                if second:
                    dve.sem_inc(s["g_vec_used"], 1)

            def stage_c(k):
                if k == 0:
                    dve.wait_ge(s["c_adj_in"], 16)
                    step(dve.tensor_scalar(m.cbias[:, :], m.cadj[:, :], 0.0, 1.0, ALU.is_gt, ALU.subtract))
                    step(dve.tensor_scalar(m.cbias[:, :], m.cbias[:, :], -MASKED, None, ALU.mult))
                if k in (5, 6):
                    half = k - 5
                    dve.wait_ge(s["c_s_ps"], half + 1)
                    step(dve.scalar_tensor_tensor(out=m.catt[:, 4 * half:4 * half + 4, :],
                                                  in0=heads4((m.C0, m.C1)[half]), scalar=float(D) ** -0.5,
                                                  in1=over(m.causal[:, :], 128, 4, 128, 1),
                                                  op0=ALU.mult, op1=ALU.add))
                if k == 6:
                    dve.tensor_reduce(m.cnm[:, :], m.catt[:, :, :], AX.X, ALU.max, negate=True).then_inc(s["c_max"], 1)
                if k == 7:
                    dve.wait_ge(s["c_p"], 1)
                    dve.reciprocal(m.crs[:, :], m.csum[:, :]).then_inc(s["c_rs"], 1)
                if k == 12:
                    dve.wait_ge(s["c_wo"], 1)
                    step(dve.tensor_tensor(m.cx2[:, :], m.C0[:, 0:D], m.hand_c[:, 0, :], ALU.add))
                    moments(m.cx2[:, :], m.cst[:, :], m.cmv[:, :], s["c_var"])
                if k == 13:
                    dve.wait_ge(s["c_rstd"], 1)
                    step(normalize(m.cy[:, :], m.cx2[:, :], m.cmv, m.crstd))
                    moments(m.cy[:, :], m.cst[:, :], m.cmv[:, :], s["c_var"])
                if k == 14:
                    dve.wait_ge(s["c_rstd"], 2)
                    normalize(m.cn[:, :], m.cy[:, :], m.cmv, m.crstd).then_inc(s["c_n"], 1)
                    dve.wait_ge(s["c_n"], 1)
                    step(dve.tensor_tensor(m.cqkv[:, :], m.cn[:, :], p["g1_row"], ALU.mult))
                    dve.tensor_tensor(m.cqkv[:, :], m.cqkv[:, :], p["be1_row"], ALU.add).then_inc(s["c_qkv"], 1)
                if k in (16, 17):
                    half = k - 16
                    dve.wait_ge(s["c_g_ps"], half + 1)
                    step(dve.scalar_tensor_tensor(out=m.catt[:, 4 * half:4 * half + 4, :],
                                                  in0=heads4((m.C0, m.C1)[half]), scalar=float(GD) ** -0.5,
                                                  in1=over(m.cbias[:, :], 128, 4, 128, 1),
                                                  op0=ALU.mult, op1=ALU.add))
                if k == 17:
                    dve.tensor_reduce(m.cnm[:, :], m.catt[:, :, :], AX.X, ALU.max, negate=True).then_inc(s["c_gmax"], 1)
                if k == 18:
                    dve.wait_ge(s["c_gp"], 1)
                    step(dve.reciprocal(m.crs[:, :], m.csum[:, :]))
                if k == 21:
                    dve.wait_ge(s["c_go"], 1)
                    step(dve.tensor_tensor(m.cxp[:, :].rearrange("p (h c) -> p h c", h=GH),
                                           m.C0[:, 0:128].rearrange("p (h c) -> p h c", h=GH),
                                           over(m.crs[:, :], 128, GH, GD, 2), ALU.mult))
                    step(dve.tensor_tensor(m.cxp[:, :], m.cxp[:, :], m.cy[:, :], ALU.add))
                    moments(m.cxp[:, :], m.cst[:, :], m.cmv[:, :], s["c_var"])
                if k == 22:
                    dve.wait_ge(s["c_rstd"], 3)
                    normalize(m.cn[:, :], m.cxp[:, :], m.cmv, m.crstd).then_inc(s["c_n2"], 1)
                    step(dve.tensor_tensor(m.cres[:, :], m.cxp[:, :], m.cx2[:, :], ALU.add))
                    step(dve.tensor_tensor(m.cres[:, :], m.cres[:, :], p["b2_row"], ALU.add))
                if k == 25:
                    dve.wait_ge(s["c_mlp"], 1)
                    step(dve.tensor_tensor(m.x3_c[:, :], m.C1[:, 0:D], m.cres[:, :], ALU.add))

            def stage_d(k):
                if k == 0:
                    moments(m.x3_d[:, :], m.dst6[:, :], m.dmv[:, :], s["d_var"])
                if k == 1:
                    dve.wait_ge(s["d_rstd"], 1)
                    normalize(m.du[:, :], m.x3_d[:, :], m.dmv, m.drstd).then_inc(s["d_u"], 1)
                    step(dve.tensor_tensor(m.dres[:, :], m.x3_d[:, :], p["outb_row"], ALU.add))
                if k == 3:
                    dve.wait_ge(s["d_l_ps"], 1)
                    step(dve.tensor_tensor(m.dz[:, :, :].rearrange("p h g -> p (h g)"), m.D1[:, :], m.lbias[:, :],
                                           ALU.add))
                    step(dve.tensor_reduce(m.dnm[:, :], m.dz[:, :, :], AX.X, ALU.max, negate=True))
                    dve.tensor_tensor(m.dz[:, :, :], m.dz[:, :, :], over(m.dnm[:, :], 128, SH, SL, 2),
                                      ALU.add).then_inc(s["d_z"], 1)
                if k == 4:
                    dve.wait_ge(s["d_fx_ps"], 1)
                    dve.tensor_tensor(m.dfx[:, :, 0:SP_], m.D0[:, :].rearrange("p (h c) -> p h c", h=SH),
                                      p["bfx_row"].rearrange("p (h c) -> p h c", h=SH), ALU.add)
                    dve.wait_ge(s["d_e"], 1)
                    step(dve.tensor_reduce(m.dnm[:, :], m.dsw[:, :, :], AX.X, ALU.add))
                    step(dve.reciprocal(m.dnm[:, :], m.dnm[:, :]))
                    dve.tensor_tensor(m.dsw[:, :, :], m.dsw[:, :, :], over(m.dnm[:, :], 128, SH, SL, 2),
                                      ALU.mult).then_inc(s["d_sw"], 1)
                if k == 5:
                    dve.wait_ge(s["d_st_ps"], 1)
                    sums = [bank[0:64, 0:4 * (SP_ + 1)].rearrange("p (h c) -> p h c", h=4) for bank in (m.D0, m.D1)]
                    for half in range(2):
                        step(dve.tensor_scalar(m.dden[:, 4 * half:4 * half + 4], sums[half][:, :, SP_], EPS, None,
                                               ALU.add))
                    step(dve.reciprocal(m.dden[:, :], m.dden[:, :]))
                    for half in range(2):
                        last = dve.tensor_tensor(m.dstn[:, 4 * half:4 * half + 4, :], sums[half][:, :, 0:SP_],
                                                 over(m.dden[:, 4 * half:4 * half + 4], 64, 4, SP_, 2), ALU.mult)
                    last.then_inc(s["d_stn"], 1)
                if k == 7:
                    dve.wait_ge(s["d_dt_ps"], 1)
                    step(dve.tensor_tensor(m.ddt[:, :], m.D0[0:64, 0:2 * SH], p["dtb_row"][0:64], ALU.add))
                    step(dve.tensor_scalar(m.ddtm[:, :], m.ddt[:, :], 0.0, None, ALU.max))
                    dve.scalar_tensor_tensor(out=m.ddta[:, :], in0=m.ddt[:, :], scalar=-1.0, in1=m.ddt[:, :],
                                             op0=ALU.mult, op1=ALU.min).then_inc(s["d_dta"], 1)
                if k == 8:
                    dve.wait_ge(s["d_ln"], 1)
                    step(dve.tensor_tensor(m.ddt[:, :], m.ddta[:, :], m.ddtm[:, :], ALU.add))
                    dve.tensor_tensor(m.ddA[:, :], m.ddt[:, :], m.ea[:, :], ALU.mult).then_inc(s["d_dtA"], 1)
                    dve.wait_ge(s["d_tap"], 1)
                    for tap in (1, 0):
                        for q in range(6):
                            rows = 128 if q < 4 else 64
                            last = dve.scalar_tensor_tensor(
                                out=m.dxc[0:rows, q, :], in0=m.dxp[0:rows, q, tap:tap + SL],
                                scalar=p["convw"][0:rows, 3 * q + tap:3 * q + tap + 1],
                                in1=m.dxc[0:rows, q, :], op0=ALU.mult, op1=ALU.add)
                        if tap:
                            step(last)
                    last.then_inc(s["d_conv"], 1)
                if k == 10:
                    dve.wait_ge(s["d_DA_ps"], 1)
                    flat = m.dL[:, :, :, :].rearrange("p w h t -> p w (h t)")
                    starts = m.identrep[:, :, :].rearrange("p h t -> p (h t)")
                    dve.tensor_tensor_scan(flat[:, 0, :], m.D1[0:64, :], starts, 0.0, ALU.mult, ALU.add)
                    step(dve.tensor_tensor_scan(flat[:, 1, ::-1], m.D2[0:64, ::-1], starts[:, ::-1], 0.0,
                                                ALU.mult, ALU.add))
                    dve.wait_ge(s["d_Gs"], 1)
                    for way in range(2):
                        last = dve.tensor_tensor(m.dL[:, way, :, :], m.dL[:, way, :, :],
                                                 over(m.dG[:, :], 64, SH, SL, 1), ALU.mult)
                    step(last)
                    for way, out in enumerate((m.dMf[:, :, 1:SL + 1], m.dMb[:, :, 0:SL])):
                        last = dve.tensor_tensor(out, m.dL[:, way, :, :],
                                                 over(m.ddt[:, SH * way:SH * (way + 1)], 64, SH, SL, 2), ALU.mult)
                    last.then_inc(s["d_M"], 1)
                if k == 11:
                    dve.wait_ge(s["d_fd_ps"], 1)
                    step(dve.tensor_tensor(m.dfd[:, :], m.D0[0:64, 0:SH], p["dp_row"][0:64], ALU.add))
                if k == 12:
                    dve.wait_ge(s["d_xn"], 1)
                    step(dve.tensor_tensor(m.dyg[:, :, :], m.dxn[:, :, :], over(m.dfd[:, :], 64, SH, SP_, 2), ALU.mult))
                    dve.wait_ge(s["d_y_ps"], 1)
                    step(dve.tensor_tensor(m.dyg[:, :, :], m.D2[0:64, :].rearrange("p (h c) -> p h c", h=SH),
                                           m.dyg[:, :, :], ALU.add))
                    dve.wait_ge(s["d_silz"], 1)
                    dve.tensor_tensor(m.dyg[:, :, :], m.dyg[:, :, :],
                                      m.dstn[:, :, :], ALU.mult).then_inc(s["d_yg"], 1)
                if k == 13:
                    dve.wait_ge(s["d_rr"], 1)
                    dve.tensor_scalar(m.dyg[:, :, :], m.dyg[:, :, :], m.dss[:, 0:1], None, ALU.mult)\
                        .then_inc(s["d_ygn"], 1)
                if k == 17:
                    dve.wait_ge(s["d_f_ps"], 1)
                    dve.tensor_tensor(m.dout[:, :], m.D0[:, 0:D], m.dres[:, :], ALU.add).then_inc(s["d_out"], 1)

            def finish_weights():
                dve.tensor_scalar(m.ea[:, :], p["alog_row"][0:64], LOG_MAX, None, ALU.min).then_inc(s["fold_row"], 1)
                step(dve.tensor_scalar(m.invt[:, :], p["temp_row"], TEMP_MIN, None, ALU.max))
                step(dve.reciprocal(m.invt[:, :], m.invt[:, :]))
                for ident in (m.identf, m.identb):
                    step(dve.tensor_copy(ident[:, :], m.ident[0:64, 0:64]))
                step(dve.memset(m.identf[:, 0:1], 0.0))
                step(dve.memset(m.identb[:, SL - 1:SL], 0.0))
                step(dve.tensor_copy(m.identrep[:, :, :], over(m.ident[0:64, 0:64], 64, SH, SL, 1)))
                by_head = over(m.invt[:, :], 128, SH, SL, 2)
                by_slice = over(p["bslice_row"], 128, SH, SL, 1)
                wslice = m.wslice[:, :].rearrange("p (h g) -> p h g", h=SH)
                lbias = m.lbias[:, :].rearrange("p (h g) -> p h g", h=SH)
                step(dve.tensor_tensor(wslice, m.D0[:, :].rearrange("p (h g) -> p h g", h=SH), by_head, ALU.mult))
                step(dve.tensor_tensor(lbias, m.D1[:, :].rearrange("p (h g) -> p h g", h=SH), by_slice, ALU.add))
                step(dve.tensor_tensor(lbias, lbias, by_head, ALU.mult))

            if do_g:
                dve.tensor_copy(m.idx_g[:, :], m.idx_a[:, :]).then_inc(s["hand_idx"], 1)
                dve.tensor_copy(m.w_g[:, :], m.w_a[:, :]).then_inc(s["hand_w"], 1)
            if do_d:
                step(dve.tensor_copy(m.x3_d[:, :], m.x3_c[:, :]))
            if do_c:
                dve.tensor_copy(m.hand_c[:, :, :], m.hand_g[:, :, :]).then_inc(s["hand_h2T"], 1)
                dve.wait_ge(s["hand_h2T"], 1)
            if do_g:
                step(dve.tensor_copy(m.hand_g[:, :, :], m.hand_a[:, :, :]))
            for slot in range(SLOTS):
                if do_a:
                    stage_a(slot)
                if finish and slot == FOLD:
                    finish_weights()
                if do_g and slot == 8:
                    if do_c:
                        dve.wait_ge(s["g_carried"], CARRIED)
                    dve.tensor_copy(m.idx_l[:, :], m.idx_g[:, IN_TURN * GROUP:]).then_inc(s["hand_idx"], 1)
                if do_c and slot in c_at:
                    stage_c(c_at[slot])
                if do_d and slot in d_at:
                    stage_d(d_at[slot])
                if do_g:
                    stage_g(slot)


def two_layers(nc, x, adj, table, params, factors, out, graphs=B):
    dram = {"x": x, "adj": adj, "table": table, "params": params, "factors": factors, "out": out}
    with ExitStack() as ctx:
        m = lay_out_memory(nc, ctx)
        s = {name: ctx.enter_context(nc.semaphore(name)) for name in SIGNALS}
        s["gathered"] = [ctx.enter_context(nc.semaphore(f"gathered{i}")) for i in range(RING)]
        first, last = s["cols_in"].num, s["d_stored"].num
        assert last - first + 1 == len(SIGNALS)

        def again():
            nc.vector.sem_clear(range(first, last + 1))
            nc.all_engine_barrier(sem_only=True)

        set_up(nc, m, s, dram)
        turn(nc, m, s, dram, a=0, fold=True)
        again()
        turn(nc, m, s, dram, a=1, g=0, finish=True)
        again()
        turn(nc, m, s, dram, a=2, g=1, c=0)
        again()
        if graphs > 3:
            with nc.Fori(3, graphs) as a:
                turn(nc, m, s, dram, a=a, g=a - 1, c=a - 2, d=a - 3)
                again()
        turn(nc, m, s, dram, g=graphs - 1, c=graphs - 2, d=graphs - 3)
        again()
        turn(nc, m, s, dram, c=graphs - 1, d=graphs - 2)
        again()
        turn(nc, m, s, dram, d=graphs - 1)


def lay_out_inputs(i):
    import numpy as np

    f = {k: np.asarray(v) for k, v in i.items()}

    def chunks(w, n):
        return w.reshape(n, -1, w.shape[-1]).transpose(1, 0, 2).reshape(w.shape[0] // n, -1)

    def rows(v, n=128):
        return np.broadcast_to(v.reshape(1, -1), (n, v.size))

    def fill(table, parts, made):
        cols = []
        for name, width in table:
            v = made[name]
            assert v.shape[1] == width, (name, v.shape, width)
            if v.shape[0] < parts:
                v = np.concatenate([v, np.zeros((parts - v.shape[0], width), v.dtype)])
            cols.append(v)
        return np.ascontiguousarray(np.concatenate(cols, 1))

    def conv(w):
        zero = np.zeros((64, w.shape[1]), w.dtype)
        w = np.concatenate([w[:DI + NS], zero, w[DI + NS:], zero])
        return chunks(w, 6)

    params = fill(PARAMS, 128, {
        "a_cols": np.stack([f[f"L0_gnn_a{k}"] for k in range(4)], 1),
        "wq": f["L0_ffn_Wq"],
        "wo": chunks(f["L0_ffn_Wo"], HEADS),
        "gb_cols": np.stack([f[f"L1_gnn_{k}"] for k in ("gamma1", "beta1", "gamma2", "beta2")], 1),
        "b1_cols": f["L1_gnn_b1"].reshape(FF, 128).T,
        "g1_row": rows(f["L1_gnn_gamma1"]), "be1_row": rows(f["L1_gnn_beta1"]),
        "b2_row": rows(f["L1_gnn_b2"]), "outb_row": rows(f["L1_ffn_out_b"]),
        "w1": f["L1_gnn_W1"], "w2": chunks(f["L1_gnn_W2"], FF),
        "wfx": f["L1_ffn_W_fx"].T, "bfx_row": rows(f["L1_ffn_b_fx"]),
        "bslice_row": rows(f["L1_ffn_b_slice"]), "temp_row": rows(f["L1_ffn_temperature"]),
        "inw": chunks(f["L1_ffn_hy_in_w"].T, KC),
        "convw": conv(f["L1_ffn_hy_conv_w"]), "convb": conv(f["L1_ffn_hy_conv_b"][:, None]),
        "dtb_row": rows(np.concatenate([f["L1_ffn_hy_dt_bias"]] * 2)),
        "alog_row": rows(np.concatenate([f["L1_ffn_hy_A_log"]] * 2)),
        "fcd": chunks(f["L1_ffn_hy_fcD_w"].T, KC), "dp_row": rows(f["L1_ffn_hy_D"]),
        "normw": chunks(f["L1_ffn_hy_norm_w"][:, None], KC), "hyout": chunks(f["L1_ffn_hy_out_w"].T, KC),
        "outw": chunks(f["L1_ffn_out_w"].T, KC),
    })
    factors = fill(FACTORS, 64, {
        "wqpk_t": f["L0_ffn_Wq_pk"].T.reshape(16, DK, D).transpose(1, 0, 2).reshape(DK, -1),
        "keys_t": f["L0_ffn_pk_keys"].transpose(3, 0, 2, 1).reshape(DK, -1),
        "wx": chunks(f["L1_ffn_W_x"], SH), "bx": f["L1_ffn_b_x"].reshape(SH, SP_).T,
        "wslice_t": f["L1_ffn_W_slice"].T,
    })
    table = np.concatenate([f["L0_ffn_keys_table"], f["L0_ffn_values_table"]], 1)
    return {"x": f["x"], "adj": f["adj"], "table": table, "params": params, "factors": factors}


def kernel(**inputs):
    import concourse.bacc as _bacc
    from concourse.bass_utils import run_bass_kernel_spmd as _run

    nc = _bacc.Bacc("TRN2", target_bir_lowering=False, num_devices=1)
    arrays = lay_out_inputs(inputs)
    args = {n: nc.dram_tensor(n, a.shape, mybir.dt.from_np(a.dtype), kind="ExternalInput").ap()
            for n, a in arrays.items()}
    out = nc.dram_tensor("out", (B, T, D), F32, kind="ExternalOutput").ap()
    two_layers(nc, out=out, **args)
    return _run(nc, [arrays], core_ids=[0]).results[0]["out"]
```
